# Optimizing a Trainium2 kernel written in Bass

```python
import numpy as np
import jax
import jax.numpy as jnp

def _softmax(x, axis=-1):
    return jax.nn.softmax(x, axis=axis)

def _gelu(x):
    return jax.nn.gelu(x, approximate=True)

def _silu(x):
    return jax.nn.silu(x)

def _sigmoid(x):
    return jax.nn.sigmoid(x)

def _layernorm(x, axis=-1, eps=1e-05):
    m = jnp.mean(x, axis=axis, keepdims=True)
    v = jnp.var(x, axis=axis, keepdims=True)
    return (x - m) / jnp.sqrt(v + eps)

def _scatter_add(tgt, idx, src, axis=0):
    return tgt.at[idx].add(src)

def _segment_sum(src, seg, n):
    return jax.ops.segment_sum(src, seg, n)
kernel_name = 'mk_gnn_preln_d4_gnn_r8_584d30'

def setup_inputs(seed: int=0):
    np.random.seed(seed)
    _w = jnp.asarray

    def _rec_inputs():
        import jax
        import jax.numpy as jnp
        _gk = jax.random.key(seed)
        x = -8.776e-05 + 1 * jax.random.normal(jax.random.fold_in(_gk, 1), (12500, 128), jnp.float32)
        src = jax.random.randint(jax.random.fold_in(_gk, 2), (200000,), 0, 12500, jnp.int32)
        dst = jax.random.randint(jax.random.fold_in(_gk, 3), (200000,), 0, 12500, jnp.int32)
        _o = jnp.argsort(dst, stable=True)
        src = src[_o]
        dst = dst[_o]
        edge_attr_128 = -4.21973e-05 + 0.999841 * jax.random.normal(jax.random.fold_in(_gk, 12), (200000, 128), jnp.float32)
        edge_attr_64 = -0.000128692 + 0.999872 * jax.random.normal(jax.random.fold_in(_gk, 13), (200000, 64), jnp.float32)
        edge_type_8 = jax.random.randint(jax.random.fold_in(_gk, 15), (200000,), 0, 8, jnp.int32)
        return (x, src, dst, edge_attr_128, edge_attr_64, edge_type_8)
    x, src, dst, edge_attr_128, edge_attr_64, edge_type_8 = _rec_inputs()

    def _L0_gnn_setup():
        import jax, jax.numpy as jnp
        import numpy as np
        N_NODES = 5000
        N_EDGES = 80000
        NODE_D = 128
        EDGE_D = 64
        OUT_D = 128
        key = jax.random.key(seed)
        ks = jax.random.split(key, 8)
        return {'node_features': jax.random.normal(ks[0], (N_NODES, NODE_D), dtype=jnp.float32), 'edge_features': jax.random.normal(ks[1], (N_EDGES, EDGE_D), dtype=jnp.float32), 'src': jax.random.randint(ks[2], (N_EDGES,), 0, N_NODES, dtype=jnp.int32), 'dst': jax.random.randint(ks[3], (N_EDGES,), 0, N_NODES, dtype=jnp.int32), 'W_msg_w': jax.random.normal(ks[4], (OUT_D, NODE_D + EDGE_D), dtype=jnp.float32) * 0.05, 'W_msg_b': jax.random.normal(ks[5], (OUT_D,), dtype=jnp.float32) * 0.05, 'W_apply_w': jax.random.normal(ks[6], (OUT_D, OUT_D + NODE_D), dtype=jnp.float32) * 0.05, 'W_apply_b': jax.random.normal(ks[7], (OUT_D,), dtype=jnp.float32) * 0.05}
    _L0_gnn_all = _L0_gnn_setup()
    _L0_gnn_in = {k: v for k, v in _L0_gnn_all.items() if k in ('W_msg_w', 'W_msg_b', 'W_apply_w', 'W_apply_b')}
    del _L0_gnn_all

    def _L1_gnn_setup():
        import jax, jax.numpy as jnp
        import numpy as np
        N_NODES = 12500
        N_EDGES = 75000
        D = 128
        key = jax.random.key(seed)
        ks = jax.random.split(key, 6)
        node_feat = jax.random.normal(ks[0], (N_NODES, D), dtype=jnp.float32)
        edge_feat = jax.random.normal(ks[1], (N_EDGES, D), dtype=jnp.float32)
        src = jax.random.randint(ks[2], (N_EDGES,), 0, N_NODES, dtype=jnp.int32)
        dst = jax.random.randint(ks[3], (N_EDGES,), 0, N_NODES, dtype=jnp.int32)
        lim = 1.0 / np.sqrt(D)
        W1 = jax.random.uniform(ks[4], (D, D), jnp.float32, -lim, lim)
        b1 = jnp.zeros((D,), jnp.float32)
        W2 = jax.random.uniform(ks[5], (D, D), jnp.float32, -lim, lim)
        b2 = jnp.zeros((D,), jnp.float32)
        return {'node_feat': node_feat, 'edge_feat': edge_feat, 'src': src, 'dst': dst, 'W1': W1, 'b1': b1, 'W2': W2, 'b2': b2}
    _L1_gnn_all = _L1_gnn_setup()
    _L1_gnn_in = {k: v for k, v in _L1_gnn_all.items() if k in ('W1', 'b1', 'W2', 'b2')}
    del _L1_gnn_all

    def _L2_gnn_setup():
        import jax, jax.numpy as jnp
        import numpy as np
        N = 6250
        E = 100000
        IN_DIM = 128
        OUT_DIM = 128
        HEADS = 4
        HEAD_DIM = OUT_DIM // HEADS
        key = jax.random.key(seed)
        k1, k2, k3, k4 = jax.random.split(key, 4)
        x = jax.random.normal(k1, (N, IN_DIM), dtype=jnp.float32)
        edge_index = jax.random.randint(k2, (2, E), 0, N, dtype=jnp.int32)
        W = jax.random.normal(k3, (OUT_DIM, IN_DIM), dtype=jnp.float32) * (1.0 / np.sqrt(IN_DIM))
        a_w = jax.random.normal(k4, (2 * HEAD_DIM,), dtype=jnp.float32) * (1.0 / np.sqrt(2 * HEAD_DIM))
        return {'x': x, 'edge_index': edge_index, 'W': W, 'a_w': a_w}
    _L2_gnn_all = _L2_gnn_setup()
    _L2_gnn_in = {k: v for k, v in _L2_gnn_all.items() if k in ('W', 'a_w')}
    del _L2_gnn_all

    def _L3_gnn_setup():
        import jax, jax.numpy as jnp
        import numpy as np
        N_NODES = 12500
        N_REL = 8
        EMB = 128
        N_EDGES = 200000
        key = jax.random.key(seed)
        k1, k2, k3, k4, k5 = jax.random.split(key, 5)
        node_emb = jax.random.normal(k1, (N_NODES, EMB), dtype=jnp.float32)
        weights = jax.random.normal(k2, (N_REL, EMB, EMB), dtype=jnp.float32) / np.sqrt(EMB)
        src = jax.random.randint(k3, (N_EDGES,), 0, N_NODES, dtype=jnp.int32)
        rel = jax.random.randint(k4, (N_EDGES,), 0, N_REL, dtype=jnp.int32)
        dst = jax.random.randint(k5, (N_EDGES,), 0, N_NODES, dtype=jnp.int32)
        return {'node_emb': node_emb, 'weights': weights, 'src': src, 'rel': rel, 'dst': dst}
    _L3_gnn_all = _L3_gnn_setup()
    _L3_gnn_in = {k: v for k, v in _L3_gnn_all.items() if k in ('weights',)}
    del _L3_gnn_all
    return {'x': x, 'src': src, 'dst': dst, 'edge_attr_128': edge_attr_128, 'edge_attr_64': edge_attr_64, 'edge_type_8': edge_type_8, 'L0_gnn_W_msg_w': _L0_gnn_in['W_msg_w'], 'L0_gnn_W_msg_b': _L0_gnn_in['W_msg_b'], 'L0_gnn_W_apply_w': _L0_gnn_in['W_apply_w'], 'L0_gnn_W_apply_b': _L0_gnn_in['W_apply_b'], 'L1_gnn_W1': _L1_gnn_in['W1'], 'L1_gnn_b1': _L1_gnn_in['b1'], 'L1_gnn_W2': _L1_gnn_in['W2'], 'L1_gnn_b2': _L1_gnn_in['b2'], 'L2_gnn_W': _L2_gnn_in['W'], 'L2_gnn_a_w': _L2_gnn_in['a_w'], 'L3_gnn_weights': _L3_gnn_in['weights']}

def reference(x, src, dst, edge_attr_128, edge_attr_64, edge_type_8, L0_gnn_W_msg_w, L0_gnn_W_msg_b, L0_gnn_W_apply_w, L0_gnn_W_apply_b, L1_gnn_W1, L1_gnn_b1, L1_gnn_W2, L1_gnn_b2, L2_gnn_W, L2_gnn_a_w, L3_gnn_weights):
    import jax
    import jax.numpy as jnp

    def _L0_gnn_ref(node_features, edge_features, src, dst, W_msg_w, W_msg_b, W_apply_w, W_apply_b):
        import jax, jax.numpy as jnp
        import numpy as np
        N_NODES = 5000
        N_EDGES = 80000
        NODE_D = 128
        EDGE_D = 64
        OUT_D = 128
        n_nodes = node_features.shape[0]
        msg_in = jnp.concatenate([node_features[src], edge_features], axis=-1)
        m = jax.nn.relu(msg_in @ W_msg_w.T + W_msg_b)
        h_neigh = jax.ops.segment_sum(m, dst, num_segments=n_nodes)
        apply_in = jnp.concatenate([node_features, h_neigh], axis=-1)
        return jax.nn.relu(apply_in @ W_apply_w.T + W_apply_b)

    def _L1_gnn_ref(node_feat, edge_feat, src, dst, W1, b1, W2, b2):
        import jax, jax.numpy as jnp
        import numpy as np
        N_NODES = 12500
        N_EDGES = 75000
        D = 128
        m = node_feat[src] + edge_feat
        neigh = jax.ops.segment_sum(m, dst, num_segments=node_feat.shape[0])
        h = 2.0 * node_feat + neigh
        h = h @ W1 + b1
        h = jnp.where(h > 0, h, 0.01 * h)
        return h @ W2 + b2

    def _L2_gnn_ref(x, edge_index, W, a_w):
        import jax, jax.numpy as jnp
        import numpy as np
        N = 6250
        E = 100000
        IN_DIM = 128
        OUT_DIM = 128
        HEADS = 4
        HEAD_DIM = OUT_DIM // HEADS
        n = x.shape[0]
        Wx = (x @ W.T).reshape(n, HEADS, HEAD_DIM)
        src, dst = (edge_index[0], edge_index[1])
        Wx_src = Wx[src]
        Wx_dst = Wx[dst]
        a_src, a_dst = (a_w[:HEAD_DIM], a_w[HEAD_DIM:])
        e = jnp.einsum('ehd,d->eh', Wx_src, a_src) + jnp.einsum('ehd,d->eh', Wx_dst, a_dst)
        e = jax.nn.leaky_relu(e, negative_slope=0.2)
        e_max = jax.ops.segment_max(e, dst, num_segments=n)
        e_exp = jnp.exp(e - e_max[dst])
        denom = jax.ops.segment_sum(e_exp, dst, num_segments=n)
        alpha = e_exp / (denom[dst] + 1e-08)
        weighted = alpha[..., None] * Wx_src
        out = jax.ops.segment_sum(weighted, dst, num_segments=n)
        return jax.nn.elu(out.reshape(n, OUT_DIM))

    def _L3_gnn_ref(node_emb, weights, src, rel, dst):
        import jax, jax.numpy as jnp
        import numpy as np
        N_NODES = 12500
        N_REL = 8
        EMB = 128
        N_EDGES = 200000
        n, e = node_emb.shape
        r = weights.shape[0]
        fr = src + n * rel
        vals = jnp.ones(src.shape[0], dtype=node_emb.dtype)
        rowsum = jax.ops.segment_sum(vals, fr, num_segments=r * n)
        vals = vals / rowsum[fr]
        msgs = vals[:, None] * node_emb[dst]
        agg = jax.ops.segment_sum(msgs, fr, num_segments=r * n)
        agg = agg.reshape(r, n, e)
        out = jnp.einsum('rij,rnj->ni', weights, agg)
        return jax.nn.relu(out)
    edge_index = jnp.stack([src, dst])
    h = jnp.maximum(_layernorm(x, axis=-1), 0.0)
    x = x + _L0_gnn_ref(h, edge_attr_64, src, dst, L0_gnn_W_msg_w, L0_gnn_W_msg_b, L0_gnn_W_apply_w, L0_gnn_W_apply_b)
    h = jnp.maximum(_layernorm(x, axis=-1), 0.0)
    x = x + _L1_gnn_ref(h, edge_attr_128, src, dst, L1_gnn_W1, L1_gnn_b1, L1_gnn_W2, L1_gnn_b2)
    h = jnp.maximum(_layernorm(x, axis=-1), 0.0)
    x = x + _L2_gnn_ref(h, edge_index, L2_gnn_W, L2_gnn_a_w)
    h = jnp.maximum(_layernorm(x, axis=-1), 0.0)
    x = x + _L3_gnn_ref(h, L3_gnn_weights, src, edge_type_8, dst)
    return x

_drawn_inputs = setup_inputs


def setup_inputs(seed=0):
    import zlib

    import numpy as np

    out = dict(_drawn_inputs(seed))
    spreads = {'L1_gnn_b1': (0.0, 0.708), 'L1_gnn_b2': (0.0, 0.27)}
    factors = {'L2_gnn_a_w': 8.0}
    for name, (base, spread) in spreads.items():
        noise = np.random.default_rng([zlib.crc32(name.encode()), seed]).standard_normal(out[name].shape)
        drawn = base * np.exp(spread * noise) if base else spread * noise
        out[name] = jnp.asarray(drawn.astype(out[name].dtype))
    for name, factor in factors.items():
        out[name] = (out[name] * factor).astype(out[name].dtype)
    return out
```

```python
from contextlib import ExitStack

import concourse.bass as bass
from concourse import mybir

F32 = mybir.dt.float32
BF16 = mybir.dt.bfloat16
I32 = mybir.dt.int32
ALU = mybir.AluOpType
ACT = mybir.ActivationFunctionType
AX = mybir.AxisListType

P = 128
N, E, D, DE = 12500, 200000, 128, 64
HEADS, HD, REL = 4, 32, 8
NT = -(-N // P)
TAIL = N - (NT - 1) * P
NPAD = NT * P
STEPS = E // P
LONG = E - STEPS * P
K = 11
NB = STEPS // K
W = (NB + 2) * K
KN = 7
NNB = NT // KN
assert NB * K == STEPS and NB % 2 == 0 and NNB * KN == NT and NNB % 2 == 0
HW = HD + 2
AW = HEADS * HW
RSHIFT = 14
assert N <= 1 << RSHIFT
FAR = 1e30
SLOPE = 0.2
EPS = 1e-5
GK = [(g, min(g + 4, K)) for g in range(0, K, 4)]
GN = [(g, min(g + 4, KN)) for g in range(0, KN, 4)]


def batches(eng, count, body):
    body(0, 0)
    body(0, 1)
    with eng.Fori(1, count // 2) as i:
        body(i, 0)
        body(i, 1)


class Line:

    def __init__(self, eng, sem):
        self.eng, self.sem, self.base, self.n = eng, sem, 0, 0

    def at(self, base):
        self.base, self.n = base, 0

    def __call__(self, ins):
        ins.then_inc(self.sem, 1)
        self.n += 1
        self.eng.wait_ge(self.sem, self.base + self.n)


def chunked(rows):
    cut = LONG * (STEPS + 1)
    return (rows[0:cut].rearrange("(p t) r -> p t r", t=STEPS + 1),
            rows[cut:E].rearrange("(p t) r -> p t r", t=STEPS))


def nodes(rows):
    return rows.rearrange("(j p) d -> p j d", p=P)


class Core:

    def __init__(self, nc, ctx, shared=None):
        self.nc, self.ctx, self.sems, self.shared = nc, ctx, [], shared

    def sem(self, name):
        self.sems.append(self.ctx.enter_context(self.nc.semaphore(name)))
        return self.sems[-1]

    def soft(self, name):
        return self.shared.enter_context(self.nc.semaphore(name))

    def sb(self, name, shape, dt=F32):
        return self.ctx.enter_context(self.nc.sbuf_tensor(name, shape, dt))

    def ps(self, name, shape, dt=F32):
        return self.ctx.enter_context(self.nc.psum_tensor(name, shape, dt))

    def phase(self):
        return PhaseScope(self.nc, self.shared)


class PhaseScope:

    def __init__(self, nc, shared):
        self.nc, self.shared = nc, shared

    def __enter__(self):
        self.ctx = ExitStack()
        self.ctx.__enter__()
        self.core = Core(self.nc, self.ctx, self.shared)
        return self.core

    def __exit__(self, kind, *rest):
        if kind is None:
            with self.nc.Block() as block:
                @block.gpsimd
                def _(pool):
                    for sem in self.core.sems:
                        pool.sem_clear(sem)
        return self.ctx.__exit__(kind, *rest)


def setup_phase(nc, top, g, dram):
    with top.phase() as c, nc.Block() as block:
        typ = c.sb("typ", [P, W], I32)
        tmp = c.sb("digits_tmp", [P, W], I32)
        zero = c.sb("zero_rows", [P, W])
        s_zero = c.sem("su_zeroed")
        s_idx = c.sem("su_indices_loaded")
        s_x = c.sem("su_x_loaded")
        s_const = c.sem("su_constants")
        s_v = c.sem("su_vector_line")
        s_z = c.sem("su_zero_rows_written")
        line_sem = c.sem("su_pool_line")

        @block.gpsimd
        def _(pool):
            line = Line(pool, line_sem)
            for t in (g.src, g.dst, typ):
                pool.memset(t[:, STEPS:W], 0).then_inc(s_zero, 1)
            pool.memset(g.x[:, NT - 1, :], 0.0).then_inc(s_zero, 1)
            line(pool.memset(g.ones[:, :], 1.0))
            line(pool.memset(g.ident[:, :], 0.0))
            line(pool.memset(g.identb[:, :], 0.0))
            for m in (g.ident, g.identb):
                line(pool.affine_select(out=m[:, :], in_=m[:, :], compare_op=ALU.not_equal, fill=1.0,
                                        base=0, pattern=[[-1, P]], channel_multiplier=1))
            line(pool.affine_select(out=g.before[:, :], in_=g.ones[:, :], compare_op=ALU.is_gt, fill=0.0,
                                    base=0, pattern=[[1, P]], channel_multiplier=-1))
            line(pool.affine_select(out=g.upto[:, :], in_=g.ones[:, :], compare_op=ALU.is_ge, fill=0.0,
                                    base=0, pattern=[[1, P]], channel_multiplier=-1))
            line(pool.affine_select(out=g.after[:, :], in_=g.ones[:, :], compare_op=ALU.is_gt, fill=0.0,
                                    base=0, pattern=[[-1, P]], channel_multiplier=1))
            line(pool.iota(g.row[:, :], [[1, P]], base=0, channel_multiplier=0,
                           allow_small_or_imprecise_dtypes=True))
            line(pool.iota(g.part[:, :], [[0, 1]], base=0, channel_multiplier=1,
                           allow_small_or_imprecise_dtypes=True))
            line(pool.iota(g.trash[:, :], [[0, 1]], base=E, channel_multiplier=1))
            pool.sem_inc(s_const, 1)

        @block.sync
        def _(sp):
            sp.wait_ge(s_zero, 4)
            for t, rows in ((g.src, dram.src), (g.dst, dram.dst), (typ, dram.edge_type_8)):
                long, short = chunked(rows.rearrange("(e o) -> e o", o=1))
                sp.dma_start(t[0:LONG, 0:STEPS + 1], long[:, :, 0]).then_inc(s_idx, 16)
                sp.dma_start(t[LONG:P, 0:STEPS], short[:, :, 0]).then_inc(s_idx, 16)
            sp.dma_start(g.x[:, 0:NT - 1, :], nodes(dram.x[0:(NT - 1) * P, :])).then_inc(s_x, 16)
            sp.dma_start(g.x[0:TAIL, NT - 1, :], dram.x[(NT - 1) * P:N, :]).then_inc(s_x, 16)
            sp.wait_ge(s_v, 1)
            zero_rows = dram.dst_terms[0:E].rearrange("e h -> (e h)").rearrange("(p w) -> p w", p=P)
            width = zero_rows.shape[1]
            piece = zero.shape[1]
            for at in range(0, width, piece):
                n = min(piece, width - at)
                sp.dma_start(zero_rows[:, at:at + n],
                             zero[:, 0:n]).then_inc(s_z, 16)
            sp.wait_ge(s_z, 16 * -(-width // piece))
            sp.wait_ge(s_x, 32)

        @block.vector
        def _(dve):
            line = Line(dve, s_v)
            line(dve.memset(zero[:, :], 0.0))
            dve.wait_ge(s_idx, 6 * 16)
            line(dve.memset(g.keep[:, 0:1], 0.0))
            line(dve.tensor_tensor(g.keep[:, 1:W], g.dst[:, 1:W], g.dst[:, 0:W - 1], ALU.is_equal))
            for t, lo, hi in ((g.src, g.src_lo, g.src_hi), (g.dst, g.dst_lo, g.dst_hi)):
                line(dve.tensor_scalar(tmp[:, :], t[:, :], P - 1, None, ALU.bitwise_and))
                line(dve.tensor_copy(lo[:, :], tmp[:, :]))
                line(dve.tensor_scalar(tmp[:, :], t[:, :], 7, None, ALU.logical_shift_right))
                line(dve.tensor_copy(hi[:, :], tmp[:, :]))
            for word, (stride, ids) in enumerate(((NPAD, g.dst), (1 << RSHIFT, g.src))):
                line(dve.scalar_tensor_tensor(out=g.pay[:, :, word], in0=typ[:, :], scalar=float(stride), in1=ids[:, :],
                                              op0=ALU.mult, op1=ALU.add))
            dve.wait_ge(s_const, 1)
            line(dve.tensor_copy(g.rowb[:, :], g.row[:, :]))
            line(dve.tensor_scalar(g.chunk_start[:, :], g.part[:, :], float(LONG), None, ALU.min))
            line(dve.scalar_tensor_tensor(out=g.chunk_start[:, :], in0=g.part[:, :], scalar=float(STEPS),
                                          in1=g.chunk_start[:, :], op0=ALU.mult, op1=ALU.add))


def boundary_phase(nc, top, g, tag, ids, ends, seg):
    with top.phase() as c, nc.Block() as block:
        same = c.sb(f"{tag}_same", [P, STEPS + 1])
        count = c.sb(f"{tag}_count", [P, 1])
        diag = c.sb(f"{tag}_diag", [P, 2, P])
        spread = c.ps(f"{tag}_spread", [P, 2, P])
        s_v = c.sem(f"{tag}_vector_line")
        s_diag = c.sem(f"{tag}_diagonals")
        s_row = c.sem(f"{tag}_rows_spread")

        @block.vector
        def _(dve):
            line = Line(dve, s_v)
            line(dve.tensor_copy(seg.first[:, :], ids[:, 0:1]))
            line(dve.tensor_copy(seg.last[0:LONG, :], ids[0:LONG, STEPS:STEPS + 1]))
            line(dve.tensor_copy(seg.last[LONG:P, :], ids[LONG:P, STEPS - 1:STEPS]))
            dve.tensor_scalar(diag[:, 0, :], g.ident[:, :], seg.first[:, 0:1], None, ALU.mult).then_inc(s_diag, 1)
            dve.tensor_scalar(diag[:, 1, :], g.ident[:, :], seg.last[:, 0:1], None, ALU.mult).then_inc(s_diag, 1)
            line(dve.tensor_scalar(same[:, :], ids[:, 0:STEPS + 1], seg.first[:, 0:1], None, ALU.is_equal))
            line(dve.memset(same[LONG:P, STEPS:STEPS + 1], 0.0))
            line(dve.tensor_reduce(count[:, :], same[:, :], AX.X, ALU.add))
            line(dve.scalar_tensor_tensor(out=seg.first_end[:, :], in0=count[:, :], scalar=-1.0,
                                          in1=g.chunk_start[:, :], op0=ALU.add, op1=ALU.add))
            dve.wait_ge(s_row, 1)
            line(dve.scalar_tensor_tensor(out=seg.carry_mask[:, :], in0=spread[:, 0, :], scalar=seg.last[:, 0:1],
                                          in1=g.before[:, :], op0=ALU.is_equal, op1=ALU.mult))
            line(dve.scalar_tensor_tensor(out=seg.carry_mask_t[:, :], in0=spread[:, 1, :], scalar=seg.first[:, 0:1],
                                          in1=g.after[:, :], op0=ALU.is_equal, op1=ALU.mult))

        @block.tensor
        def _(pe):
            pe.wait_ge(s_diag, 2)
            pe.matmul(spread[:, 0, :], g.ones[:, :], diag[:, 0, :], start=True, stop=True)
            pe.matmul(spread[:, 1, :], g.ones[:, :], diag[:, 1, :], start=True, stop=True).then_inc(s_row, 1)


def norm_stats(line, act_order, g, stats_ready=None):
    dve = line.eng
    st = g.stats
    line(dve.tensor_tensor(g.mean[:, :], st[:, :, 1], st[:, :, 4], ALU.add))
    line(dve.tensor_tensor(g.scale[:, :], st[:, :, 1], st[:, :, 4], ALU.subtract))
    line(dve.scalar_tensor_tensor(out=g.scale[:, :], in0=g.scale[:, :], scalar=0.25, in1=g.scale[:, :],
                                  op0=ALU.mult, op1=ALU.mult))
    line(dve.tensor_tensor(g.shift[:, :], st[:, :, 2], st[:, :, 5], ALU.add))
    line(dve.scalar_tensor_tensor(out=g.scale[:, :], in0=g.shift[:, :], scalar=1.0 / D, in1=g.scale[:, :],
                                  op0=ALU.mult, op1=ALU.add))
    line(dve.tensor_scalar(g.scale[:, :], g.scale[:, :], EPS, None, ALU.add))
    act_order()
    line(dve.reciprocal(g.scale[:, :], g.shift[:, :]))
    line(dve.scalar_tensor_tensor(out=g.shift[:, :], in0=g.mean[:, :], scalar=-0.5, in1=g.scale[:, :],
                                  op0=ALU.mult, op1=ALU.mult))


def first_norm_phase(nc, top, g):
    with top.phase() as c, nc.Block() as block:
        s_st = c.sem("fn_stats")
        s_v = c.sem("fn_vector_line")
        s_root = c.sem("fn_root")

        @block.vector
        def _(dve):
            with dve.Fori(0, NT) as j:
                dve.bn_stats(g.stats[:, bass.ds(j, 1), :], g.x[:, bass.ds(j, 1), :]).then_inc(s_st, 1)
            dve.wait_ge(s_st, NT)
            norm_stats(Line(dve, s_v), lambda: dve.wait_ge(s_root, 1), g)

        @block.scalar
        def _(act):
            act.wait_ge(s_v, 6)
            nc.scalar.activation(g.shift[:, :], g.scale[:, :], ACT.Sqrt).then_inc(s_root, 1)


def project_phase(nc, top, g, tag, table, weights=None, cols=0, bias=None, out_cols=0, copy_act=None, copy_dve=None,
                  prepare=None, writes=1):
    with top.phase() as c, nc.Block() as block:
        h = c.sb(f"{tag}_h", [P, 2, KN, D])
        s_h = c.sem(f"{tag}_h_ready")
        s_w = [c.sem(f"{tag}_written{s}") for s in range(2)]

        def normalise(act, i, s):
            for k in range(KN):
                j = 2 * KN * i + s * KN + k
                nc.scalar.activation(h[:, s, k:k + 1, :], g.x[:, bass.ds(j, 1), :], ACT.Relu,
                                     bias=g.shift[:, bass.ds(j, 1)], scale=g.scale[:, bass.ds(j, 1)]).then_inc(s_h, 1)

        if weights is None:
            @block.scalar
            def _(act):
                def body(i, s):
                    if not isinstance(i, int):
                        act.wait_ge(s_w[s], i * 16)
                    normalise(act, i, s)
                batches(act, NNB, body)

            @block.sync
            def _(sp):
                def body(i, s):
                    sp.wait_ge(s_h, 2 * KN * i + (s + 1) * KN)
                    sp.dma_start(table(2 * KN * i + s * KN, KN), h[:, s, :, :]).then_inc(s_w[s], 16)
                batches(sp, NNB, body)
                for s in range(2):
                    sp.wait_ge(s_w[s], 16 * (NNB // 2))
            return

        ht = c.sb(f"{tag}_h_transposed", [P, 2, KN, D])
        out = c.sb(f"{tag}_out", [P, 2, KN, out_cols])
        tp = c.ps(f"{tag}_transposes", [P, 2, 2 * 512])
        split = D if cols < 512 else 512
        parts = [(at, min(split, cols - at), 512 * n) for n, at in enumerate(range(0, cols, split))]
        mm = c.ps(f"{tag}_products", [P, 2, 512 * len(parts)])
        s_pre = c.sem(f"{tag}_prepared")
        s_t = c.sem(f"{tag}_transposed")
        s_tc = c.sem(f"{tag}_transposes_copied")
        s_m = c.sem(f"{tag}_products_ready")
        s_e = c.sem(f"{tag}_products_copied_by_scalar")
        s_e2 = c.sem(f"{tag}_products_copied_by_vector")

        @block.scalar
        def _(act):
            def body(i, s):
                if not isinstance(i, int):
                    act.wait_ge(s_t, 2 * i + s - 1)
                normalise(act, i, s)
                if not isinstance(i, int):
                    act.wait_ge(s_w[s], i * 16 * writes)
                for k in range(KN):
                    act.wait_ge(s_m, 2 * KN * i + s * KN + k + 1)
                    copy_act(out[:, s, k, :], mm[:, (s * KN + k) % 2, :]).then_inc(s_e, 1)
            act.wait_ge(s_pre, 1)
            batches(act, NNB, body)

        @block.vector
        def _(dve):
            if prepare is not None:
                prepare(dve, out, s_pre)
            else:
                dve.sem_inc(s_pre, 1)

            def body(i, s):
                dve.wait_ge(s_t, 2 * i + s + 1)
                if not isinstance(i, int):
                    dve.wait_ge(s_m, (2 * i + s - 1) * KN)
                dve.tensor_copy(ht[:, s, :, :].rearrange("p k d -> p (k d)"), tp[:, s, 0:KN * D]).then_inc(s_tc, 1)
                if copy_dve is not None:
                    if not isinstance(i, int):
                        dve.wait_ge(s_w[s], i * 16 * writes)
                    for k in range(KN):
                        j = 2 * KN * i + s * KN + k
                        dve.wait_ge(s_m, j + 1)
                        copy_dve(out[:, s, k, :], mm[:, (s * KN + k) % 2, :], j).then_inc(s_e2, 1)
            batches(dve, NNB, body)

        @block.tensor
        def _(pe):
            def body(i, s):
                if not isinstance(i, int):
                    pe.wait_ge(s_tc, 2 * i + s - 1)
                for k in range(KN):
                    pe.wait_ge(s_h, 2 * KN * i + s * KN + k + 1)
                    ins = pe.transpose(tp[:, s, k * D:(k + 1) * D], h[:, s, k, :], g.ident[:, :])
                ins.then_inc(s_t, 1)
                pe.wait_ge(s_tc, 2 * i + s + 1)
                for k in range(KN):
                    j = 2 * KN * i + s * KN + k
                    if not isinstance(i, int) or j >= 2:
                        pe.wait_ge(s_e, j - 1)
                        if copy_dve is not None:
                            pe.wait_ge(s_e2, j - 1)
                    for at, n, bank in parts:
                        to = mm[:, (s * KN + k) % 2, bank:bank + n]
                        ins = pe.matmul(to, ht[:, s, k, :], weights[:, at:at + n], start=True, stop=bias is None)
                        if bias is not None:
                            ins = pe.matmul(to, g.ones[0:1, :], bias[0:1, at:at + n], start=False, stop=True)
                    ins.then_inc(s_m, 1)
            batches(pe, NNB, body)

        @block.sync
        def _(sp):
            def body(i, s):
                sp.wait_ge(s_e, 2 * KN * i + (s + 1) * KN)
                if copy_dve is not None:
                    sp.wait_ge(s_e2, 2 * KN * i + (s + 1) * KN)
                if writes == 1:
                    sp.dma_start(table(2 * KN * i + s * KN, KN), out[:, s, :, :]).then_inc(s_w[s], 16)
                else:
                    for k in range(KN):
                        sp.dma_start(table(2 * KN * i + s * KN + k, 1),
                                     out[:, s, k, :].rearrange("p (r d) -> p r d", r=REL)).then_inc(s_w[s], 16)
            batches(sp, NNB, body)
            for s in range(2):
                sp.wait_ge(s_w[s], 16 * writes * (NNB // 2))


class EdgePhase:

    def __init__(self, nc, top, c, g, tag, table, rows_dram, width):
        self.nc, self.g, self.tag, self.table, self.width = nc, g, tag, table, width
        self.rows_dram = rows_dram
        self.index = c.sb(f"{tag}_index", [P, 2, K], I32)
        self.gathered = c.sb(f"{tag}_gathered", [P, 2, K, width])
        self.rows = c.sb(f"{tag}_rows", [P, 2, K, width])
        self.s_index = c.sem(f"{tag}_index_staged")
        self.s_gat = [c.soft(f"{tag}_gathered{s}") for s in range(2)]
        self.s_used = c.sem(f"{tag}_gathered_used") if tag != "e0" else None
        self.s_go = c.sem(f"{tag}_gather_slot_free")
        self.s_rows = c.sem(f"{tag}_rows_summed")
        self.s_out = [c.sem(f"{tag}_rows_written{s}") for s in range(2)]

    def run(self, eng, body):
        batches(eng, NB, lambda i, s: body(i, s, K))
        body(NB // 2, 0, 1)

    def gather(self, pool):
        def body(i, s, n):
            pool.wait_ge(self.s_index, 2 * i + s + 1)
            if not isinstance(i, int) or i > 0:
                pool.wait_ge(self.s_used, 2 * i + s - 1)
            pool.sem_inc(self.s_go, 1)
            for k in range(n):
                pool.indirect_dma_start(
                    out=self.gathered[:, s, k, :], out_offset=None, in_=self.table,
                    in_offset=bass.IndirectOffsetOnAxis(ap=self.index[:, s, k:k + 1], axis=0)).then_inc(self.s_gat[s], 16)
        self.run(pool, body)

    def wait_gathered(self, eng, i, s, n):
        eng.wait_ge(self.s_gat[s], 16 * K * i + 16 * n)

    def stage_first(self, act, ids):
        for s in range(2):
            self.nc.scalar.copy(self.index[:, s, :], ids[:, s * K:(s + 1) * K]).then_inc(self.s_index, 1)

    def stage_next(self, act, ids, i, s, n):
        if n == K:
            self.nc.scalar.copy(self.index[:, s, :], ids[:, bass.ds(2 * K * i + (s + 2) * K, K)]).then_inc(self.s_index, 1)

    def wait_rows_out(self, eng, i, s):
        if not isinstance(i, int) or i > 0:
            eng.wait_ge(self.s_out[s], 32 * i)

    def write_rows(self, sp, i, s, n):
        sp.wait_ge(self.s_rows, 2 * K * i + s * K + n)
        long, short = chunked(self.rows_dram)
        sp.dma_start(long[:, bass.ds(2 * K * i + s * K, K), :], self.rows[0:LONG, s, :, :]).then_inc(self.s_out[s], 16)
        sp.dma_start(short[:, bass.ds(2 * K * i + s * K, K), :], self.rows[LONG:P, s, :, :]).then_inc(self.s_out[s], 16)

    def write_last(self, sp):
        sp.wait_ge(self.s_rows, STEPS + 1)
        long, _ = chunked(self.rows_dram)
        sp.dma_start(long[:, STEPS, :], self.rows[0:LONG, 0, 0, :]).then_inc(self.s_out[0], 16)
        sp.wait_ge(self.s_out[0], 32 * (NB // 2) + 16)
        sp.wait_ge(self.s_out[1], 32 * (NB // 2))

    def write_behind(self, sp, i, s, n, load):
        load(i, s, n)
        if isinstance(i, int) and i == 0 and s == 0:
            return
        if s:
            self.write_rows(sp, i, 0, K)
        else:
            self.write_rows(sp, i - 1, 1, K)

    def previous(self, s, k):
        return self.rows[:, s, k - 1] if k else self.rows[:, 1 - s, K - 1]

    def sum_steps(self, dve, keep_stage, i, s, n):
        for k in range(n):
            dve.scalar_tensor_tensor(out=self.rows[:, s, k], in0=self.previous(s, k), scalar=keep_stage[:, s, k:k + 1],
                                     in1=self.rows[:, s, k], op0=ALU.mult, op1=ALU.add).then_inc(self.s_rows, 1)
            dve.wait_ge(self.s_rows, 2 * K * i + s * K + k + 1)

    def keep_ends(self, dve, tail, s_tail):
        dve.tensor_copy(tail[0:LONG], self.rows[0:LONG, 0, 0]).then_inc(s_tail, 1)
        dve.tensor_copy(tail[LONG:P], self.rows[LONG:P, 1, K - 1]).then_inc(s_tail, 1)


def edge_phase_0(nc, top, g, dram):
    with top.phase() as c, nc.Block() as block:
        e = EdgePhase(nc, top, c, g, "e0", dram.table0[:, :], dram.rows[:, :], D)
        feat = c.sb("e0_features", [DE, 2, K, P])
        keep = c.sb("e0_keep", [P, 2, K])
        hot = [[c.sb(f"e0_{nm}_{dg}_hot", [P, 2, K, n], BF16) for dg, n in (("low", P), ("high", NT))]
               for nm in ("src", "dst")]
        z = c.ps("e0_messages", [P, 2, 3 * 512])
        hist = [c.ps("e0_src_histogram", [P, 512]), c.ps("e0_dst_histogram", [P, 512])]
        s_feat = [c.sem(f"e0_features_loaded{s}") for s in range(2)]
        s_msg = c.sem("e0_messages_ready")
        s_keep = c.sem("e0_keep_staged")
        s_hot = c.sem("e0_digits_hot")
        s_hist = c.sem("e0_histograms_counted")
        s_relu = c.sem("e0_relu_done")
        s_tail = c.sem("e0_tail")
        s_zero = c.sem("e0_zeroed")
        e.s_used = s_msg

        @block.gpsimd
        def _(pool):
            e.gather(pool)

        @block.sync
        def _(sp):
            def load(i, s, n):
                if not isinstance(i, int) or i > 0:
                    sp.wait_ge(s_msg, 2 * i + s - 1)
                sp.dma_start(feat[:, s, 0:n, :], dram.edge64_t[:, bass.ds(2 * K * i + s * K, n), :]).then_inc(s_feat[s], 16)
            e.run(sp, lambda i, s, n: e.write_behind(sp, i, s, n, load))
            e.write_last(sp)

        @block.scalar
        def _(act):
            e.stage_first(act, g.src)

            def body(i, s, n):
                e.wait_gathered(act, i, s, n)
                e.stage_next(act, g.src, i, s, n)
                act.wait_ge(s_msg, 2 * i + s + 1)
                e.wait_rows_out(act, i, s)
                if not isinstance(i, int) or i or s:
                    act.wait_ge(e.s_rows, 2 * K * i + (s - 1) * K + 1)
                for a, b in GK:
                    b = min(b, n)
                    if a < b:
                        ins = nc.scalar.activation(e.rows[:, s, a:b, :].rearrange("p k d -> p (k d)"),
                                                   z[:, s, a * D:b * D], ACT.Relu)
                ins.then_inc(s_relu, 1)
            act.wait_ge(s_zero, 1)
            e.run(act, body)

        @block.vector
        def _(dve):
            dve.memset(e.rows[:, 1, K - 1, :], 0.0).then_inc(s_zero, 1)
            dve.wait_ge(s_zero, 1)

            def body(i, s, n):
                b = 2 * K * i + s * K
                dve.tensor_copy(keep[:, s, 0:n], g.keep[:, bass.ds(b, n)]).then_inc(s_keep, 1)
                if not isinstance(i, int) or i > 0:
                    dve.wait_ge(s_hist, 2 * i + s - 1)
                for (lo, hi), (lo_hot, hi_hot) in zip(((g.src_lo, g.src_hi), (g.dst_lo, g.dst_hi)), hot):
                    for digit, to, m in ((lo, lo_hot, P), (hi, hi_hot, NT)):
                        dve.tensor_tensor(to[:, s, 0:n, :], digit[:, bass.ds(b, n)].unsqueeze(2).to_broadcast([P, n, m]),
                                          g.rowb[:, 0:m].unsqueeze(1).to_broadcast([P, n, m]), ALU.is_equal).then_inc(s_hot, 1)
                dve.wait_ge(s_keep, 2 * i + s + 1)
                dve.wait_ge(s_relu, 2 * i + s + 1)
                e.sum_steps(dve, keep, i, s, n)
            e.run(dve, body)
            e.keep_ends(dve, g.tail[:, 0:D], s_tail)
            dve.wait_ge(s_hist, NB + 1)
            dve.tensor_copy(g.src_hist[:, :], hist[0][:, 0:NT])
            dve.tensor_copy(g.dst_hist[:, :], hist[1][:, 0:NT])

        @block.tensor
        def _(pe):
            def body(i, s, n):
                e.wait_gathered(pe, i, s, n)
                pe.wait_ge(s_feat[s], 16 * (i + 1))
                if not isinstance(i, int) or i > 0:
                    pe.wait_ge(s_relu, 2 * i + s - 1)
                for a, b in GK:
                    b = min(b, n)
                    if a < b:
                        pe.matmul(z[:, s, a * D:b * D], g.ident[:, :],
                                  e.gathered[:, s, a:b, :].rearrange("p k d -> p (k d)"), start=True, stop=False,
                                  skip_group_check=True)
                        for k in range(a, b):
                            ins = pe.matmul(z[:, s, k * D:(k + 1) * D], feat[:, s, k, :], g.w0_edge[:, :],
                                            start=False, stop=True, skip_group_check=True)
                ins.then_inc(s_msg, 1)
                pe.wait_ge(s_hot, 8 * i + 4 * s + 4)
                q = P if n == K else LONG
                for to, (lo_hot, hi_hot) in zip(hist, hot):
                    for k in range(n):
                        first = isinstance(i, int) and i == 0 and s == 0 and k == 0
                        ins = pe.matmul(to[:, 0:NT], lo_hot[0:q, s, k, :], hi_hot[0:q, s, k, :],
                                        start=first, stop=n == 1, skip_group_check=True)
                ins.then_inc(s_hist, 1)
            e.run(pe, body)


def edge_phase_1(nc, top, g, dram):
    with top.phase() as c, nc.Block() as block:
        e = EdgePhase(nc, top, c, g, "e1", dram.table0[:, :], dram.rows[:, :], D)
        feat = c.sb("e1_features", [P, 2, K, D])
        keep = c.sb("e1_keep", [P, 2, K])
        s_feat = [c.sem(f"e1_features_loaded{s}") for s in range(2)]
        s_keep = c.sem("e1_keep_staged")
        s_tail = c.sem("e1_tail")
        s_zero = c.sem("e1_zeroed")

        @block.gpsimd
        def _(pool):
            e.gather(pool)

        @block.sync
        def _(sp):
            long, short = chunked(dram.edge_attr_128)

            def load(i, s, n):
                if not isinstance(i, int) or i > 0:
                    sp.wait_ge(e.s_used, 2 * i + s - 1)
                sp.dma_start(feat[0:LONG, s, 0:n, :], long[:, bass.ds(2 * K * i + s * K, n), :]).then_inc(s_feat[s], 16)
                if n == K:
                    sp.dma_start(feat[LONG:P, s, :, :], short[:, bass.ds(2 * K * i + s * K, n), :]).then_inc(s_feat[s], 16)
            e.run(sp, lambda i, s, n: e.write_behind(sp, i, s, n, load))
            e.write_last(sp)

        @block.scalar
        def _(act):
            e.stage_first(act, g.src)

            def body(i, s, n):
                e.wait_gathered(act, i, s, n)
                e.stage_next(act, g.src, i, s, n)
            e.run(act, body)

        @block.vector
        def _(dve):
            dve.memset(e.rows[:, 1, K - 1, :], 0.0).then_inc(s_zero, 1)
            dve.wait_ge(s_zero, 1)

            def body(i, s, n):
                dve.tensor_copy(keep[:, s, 0:n], g.keep[:, bass.ds(2 * K * i + s * K, n)]).then_inc(s_keep, 1)
                e.wait_gathered(dve, i, s, n)
                dve.wait_ge(s_feat[s], 32 * i + (32 if n == K else 16))
                e.wait_rows_out(dve, i, s)
                dve.tensor_tensor(e.rows[:, s, 0:n, :], e.gathered[:, s, 0:n, :], feat[:, s, 0:n, :],
                                  ALU.add).then_inc(e.s_used, 1)
                dve.wait_ge(s_keep, 2 * i + s + 1)
                dve.wait_ge(e.s_used, 2 * i + s + 1)
                e.sum_steps(dve, keep, i, s, n)
            e.run(dve, body)
            e.keep_ends(dve, g.tail[:, 0:D], s_tail)


def edge_phase_2(nc, top, g, dram):
    with top.phase() as c, nc.Block() as block:
        e = EdgePhase(nc, top, c, g, "e2", dram.table2[:, :], dram.rows2[:, :], AW)
        far = c.sb("e2_far_stage", [P, 2, K])
        score = c.sb("e2_scores", [P, K, HEADS])
        top_m = c.sb("e2_running_max", [P, K + 1, HEADS])
        power = c.sb("e2_exponents", [P, 2, K, HEADS])
        factor = c.sb("e2_factors", [P, 2, K, HEADS])
        kept = c.sb("e2_kept", [P, HEADS, HW])
        s_v = c.sem("e2_vector_line")
        s_pow = c.sem("e2_exponents_ready")
        s_exp = c.sem("e2_factors_ready")
        s_tail = c.sem("e2_tail")
        s_zero = c.sem("e2_zeroed")
        per_head = lambda ap: ap.rearrange("p k (h w) -> p k h w", h=HEADS)
        LINKS = 11

        @block.gpsimd
        def _(pool):
            e.gather(pool)

        @block.sync
        def _(sp):
            e.run(sp, lambda i, s, n: e.write_behind(sp, i, s, n, lambda *a: None))
            e.write_last(sp)

        @block.scalar
        def _(act):
            e.stage_first(act, g.src)

            def body(i, s, n):
                e.wait_gathered(act, i, s, n)
                e.stage_next(act, g.src, i, s, n)
                act.wait_ge(s_pow, 2 * i + s + 1)
                nc.scalar.activation(factor[:, :, 0:n, :], power[:, :, 0:n, :], ACT.Exp).then_inc(s_exp, 1)
            e.run(act, body)

        @block.vector
        def _(dve):
            dve.memset(top_m[:, :, :], 0.0).then_inc(s_zero, 1)
            dve.memset(e.rows[:, 1, K - 1, :], 0.0).then_inc(s_zero, 1)
            dve.wait_ge(s_zero, 2)
            line = Line(dve, s_v)

            def body(i, s, n):
                line.at(2 * LINKS * i + s * LINKS)
                b = 2 * K * i + s * K
                G = per_head(e.gathered[:, s, 0:n, :])
                R = per_head(e.rows[:, s, 0:n, :])
                line(dve.tensor_scalar(far[:, s, 0:n], g.keep[:, bass.ds(b, n)], -1.0, FAR, ALU.add, ALU.mult))
                line(dve.tensor_copy(top_m[:, 0, :], top_m[:, K, :]))
                e.wait_gathered(dve, i, s, n)
                line(dve.tensor_tensor(score[:, 0:n, :], G[:, :, :, HD + 1], g.sdst[:, bass.ds(b, n), :], ALU.add))
                line(dve.scalar_tensor_tensor(out=score[:, 0:n, :], in0=score[:, 0:n, :], scalar=SLOPE,
                                              in1=score[:, 0:n, :], op0=ALU.mult, op1=ALU.max))
                for h in range(HEADS):
                    line(dve.tensor_tensor_scan(top_m[:, 1:n + 1, h], far[:, s, 0:n], score[:, 0:n, h],
                                                top_m[:, 0, h:h + 1], ALU.add, ALU.max))
                line(dve.tensor_tensor(power[:, 0, 0:n, :], top_m[:, 0:n, :],
                                       far[:, s, 0:n].unsqueeze(2).to_broadcast([P, n, HEADS]), ALU.add))
                line(dve.tensor_tensor(power[:, 0, 0:n, :], power[:, 0, 0:n, :], top_m[:, 1:n + 1, :], ALU.subtract))
                dve.tensor_tensor(power[:, 1, 0:n, :], score[:, 0:n, :], top_m[:, 1:n + 1, :],
                                  ALU.subtract).then_inc(s_pow, 1)
                e.wait_rows_out(dve, i, s)
                dve.wait_ge(s_exp, 2 * i + s + 1)
                dve.tensor_tensor(R[:, :, :, 0:HD + 1].rearrange("p k h w -> p (k h) w"),
                                  G[:, :, :, 0:HD + 1].rearrange("p k h w -> p (k h) w"),
                                  factor[:, 1, 0:n, :].rearrange("p k h -> p (k h)").unsqueeze(2)
                                  .to_broadcast([P, n * HEADS, HD + 1]), ALU.mult).then_inc(e.s_used, 1)
                line(dve.tensor_copy(R[:, :, :, HD + 1], top_m[:, 1:n + 1, :]))
                dve.wait_ge(e.s_used, 2 * i + s + 1)
                for k in range(n):
                    before = e.previous(s, k).rearrange("p (h w) -> p h w", h=HEADS)
                    dve.tensor_tensor(kept[:, :, 0:HD + 1], before[:, :, 0:HD + 1],
                                      factor[:, 0, k, :].unsqueeze(2).to_broadcast([P, HEADS, HD + 1]),
                                      ALU.mult).then_inc(s_kept, 1)
                    dve.wait_ge(s_kept, 2 * K * i + s * K + k + 1)
                    dve.tensor_tensor(R[:, k, :, 0:HD + 1], R[:, k, :, 0:HD + 1], kept[:, :, 0:HD + 1],
                                      ALU.add).then_inc(e.s_rows, 1)
                    dve.wait_ge(e.s_rows, 2 * K * i + s * K + k + 1)
                assert line.n == LINKS, line.n
            s_kept = c.sem("e2_previous_scaled")
            e.run(dve, body)
            e.keep_ends(dve, g.tail, s_tail)


def edge_phase_3(nc, top, g, dram):
    with top.phase() as c, nc.Block() as block:
        e = EdgePhase(nc, top, c, g, "e3", dram.table3[:, :], dram.rows[:, :], D)
        keep = c.sb("e3_keep", [P, 2, K])
        weight = c.sb("e3_weight", [P, 2, K])
        s_keep = c.sem("e3_keep_staged")
        s_weight = c.sem("e3_weight_staged")
        s_tail = c.sem("e3_tail")
        s_zero = c.sem("e3_zeroed")

        @block.gpsimd
        def _(pool):
            e.gather(pool)

        @block.sync
        def _(sp):
            e.run(sp, lambda i, s, n: e.write_behind(sp, i, s, n, lambda *a: None))
            e.write_last(sp)

        @block.scalar
        def _(act):
            e.stage_first(act, g.pay[:, :, 0])

            def body(i, s, n):
                nc.scalar.copy(weight[:, s, 0:n], g.weight[:, bass.ds(2 * K * i + s * K, n)]).then_inc(s_weight, 1)
                e.wait_gathered(act, i, s, n)
                e.stage_next(act, g.pay[:, :, 0], i, s, n)
                e.wait_rows_out(act, i, s)
                if not isinstance(i, int) or i or s:
                    act.wait_ge(e.s_rows, 2 * K * i + (s - 1) * K + 1)
                act.wait_ge(s_weight, 2 * i + s + 1)
                for k in range(n):
                    ins = nc.scalar.activation(e.rows[:, s, k, :], e.gathered[:, s, k, :], ACT.Copy,
                                               scale=weight[:, s, k:k + 1])
                ins.then_inc(e.s_used, 1)
            act.wait_ge(s_zero, 1)
            e.run(act, body)

        @block.vector
        def _(dve):
            dve.memset(e.rows[:, 1, K - 1, :], 0.0).then_inc(s_zero, 1)
            dve.wait_ge(s_zero, 1)

            def body(i, s, n):
                dve.tensor_copy(keep[:, s, 0:n], g.keep[:, bass.ds(2 * K * i + s * K, n)]).then_inc(s_keep, 1)
                dve.wait_ge(s_keep, 2 * i + s + 1)
                dve.wait_ge(e.s_used, 2 * i + s + 1)
                e.sum_steps(dve, keep, i, s, n)
            e.run(dve, body)
            e.keep_ends(dve, g.tail[:, 0:D], s_tail)


def order_phase(nc, top, g):
    with top.phase() as c, nc.Block() as block:
        cum = c.ps("or_sums", [P, 4, 512])
        offset = c.sb("or_offset", [P, NT])
        end = c.sb("or_end", [P, NT])
        spare = c.sb("or_spare", [P, NT])
        trash = c.sb("or_trash", [P, 1])
        s_v = c.sem("or_vector_line")
        s_sum = c.sem("or_sums_ready")

        @block.tensor
        def _(pe):
            for n, hist in enumerate((g.src_hist, g.dst_hist)):
                pe.matmul(cum[:, 2 * n, 0:NT], g.upto[:, :], hist[:, :], start=True, stop=True)
                pe.matmul(cum[:, 2 * n + 1, 0:NT], g.ones[:, :], hist[:, :], start=True, stop=True).then_inc(s_sum, 1)

        @block.vector
        def _(dve):
            line = Line(dve, s_v)
            line(dve.tensor_copy(trash[:, :], g.trash[:, :]))
            for n, (hist, start, last, has) in enumerate(((g.src_hist, g.src_start, g.src_last, g.src_has),
                                                          (g.dst_hist, g.dst_start, g.dst_last, g.dst_has))):
                dve.wait_ge(s_sum, n + 1)
                line(dve.tensor_copy(end[:, :], cum[:, 2 * n + 1, 0:NT]))
                line(dve.tensor_tensor_scan(offset[:, :], g.ones[:, 0:NT], end[:, :], 0.0, ALU.mult, ALU.add))
                line(dve.tensor_tensor(offset[:, :], offset[:, :], end[:, :], ALU.subtract))
                line(dve.tensor_tensor(end[:, :], cum[:, 2 * n, 0:NT], offset[:, :], ALU.add))
                line(dve.tensor_tensor(start[:, :], end[:, :], hist[:, :], ALU.subtract))
                line(dve.tensor_scalar(last[:, :], end[:, :], -1.0, 0.0, ALU.add, ALU.max))
                line(dve.tensor_scalar(has[:, :], hist[:, :], 0.0, None, ALU.is_gt))
            line(dve.tensor_scalar(end[:, :], g.dst_start[:, :], trash[:, 0:1], None, ALU.subtract))
            line(dve.tensor_tensor(end[:, :], end[:, :], g.dst_has[:, :], ALU.mult))
            line(dve.tensor_scalar(g.term_row[:, :], end[:, :], trash[:, 0:1], None, ALU.add))


def sort_phase(nc, top, g, dram):
    with top.phase() as c, nc.Block() as block:
        row = c.sb("so_src_row", [P, 2, K, P], I32)
        pay = c.sb("so_payload", [P, 2, K, 2], I32)
        place = c.sb("so_place", [P, 2, K], I32)
        src = c.sb("so_src_stage", [P, 2, K])
        low = c.sb("so_low_hot", [P, 2, K, P], BF16)
        high = c.sb("so_high_hot", [P, 2, K, NT], BF16)
        low_t = c.sb("so_low_hot_transposed", [P, K, P])
        count = c.sb("so_counts", [P, 2, NT])
        waste = c.sb("so_waste", [P, P])
        same = c.sb("so_in_step", [P, K])
        before = c.sb("so_before", [P, K])
        flip = c.ps("so_low_flipped", [P, 2, 1024], BF16)
        table = c.ps("so_table", [P, 512])
        look = c.ps("so_looked_up", [P, 2, 512])
        s_row = [c.sem(f"so_row_loaded{s}") for s in range(2)]
        s_src = c.sem("so_src_staged")
        s_pay = c.sem("so_payload_staged")
        s_hot = c.sem("so_hot")
        s_same = c.sem("so_in_step_counted")
        s_flip = c.sem("so_flipped")
        s_low = c.sem("so_low_transposed")
        s_table = c.sem("so_table_counted")
        s_count = c.sem("so_table_copied")
        s_look = c.sem("so_lookups")
        s_before = c.sem("so_before_read")
        s_place = c.sem("so_places")
        s_sum = c.sem("so_places_summed")
        s_scat = [c.soft(f"so_scattered{s}") for s in range(2)]
        s_go = c.sem("so_scatter_go")

        def run(eng, body):
            batches(eng, NB, lambda i, s: body(i, s, K))
            body(NB // 2, 0, 1)
        later = lambda i: not isinstance(i, int) or i > 0

        @block.gpsimd
        def _(pool):
            def body(i, s, n):
                pool.wait_ge(s_pay, 2 * i + s + 1)
                pool.wait_ge(s_place, 2 * i + s + 1)
                pool.sem_inc(s_go, 1)
                for k in range(n):
                    pool.indirect_dma_start(
                        out=dram.sorted[:, :], in_=pay[:, s, k, :], in_offset=None,
                        out_offset=bass.IndirectOffsetOnAxis(ap=place[:, s, k:k + 1], axis=0)).then_inc(s_scat[s], 16)
            run(pool, body)
            pool.wait_ge(s_scat[0], 16 * K * (NB // 2) + 16)
            pool.wait_ge(s_scat[1], 16 * K * (NB // 2))

        @block.sync
        def _(sp):
            def body(i, s, n):
                if later(i):
                    sp.wait_ge(s_same, K * (2 * i + s - 1))
                sp.dma_start(row[:, s, 0:n, :].rearrange("p k q -> p (k q)"),
                             dram.src_t[bass.ds(2 * K * i + s * K, n), :].rearrange("k q -> (k q)")
                             .partition_broadcast(P)).then_inc(s_row[s], 16)
            run(sp, body)

        @block.scalar
        def _(act):
            def body(i, s, n):
                b = 2 * K * i + s * K
                if later(i):
                    act.wait_ge(s_scat[s], 16 * K * i)
                nc.scalar.copy(pay[:, s, 0:n, :], g.pay[:, bass.ds(b, n), :]).then_inc(s_pay, 1)
                act.wait_ge(s_flip, 2 * i + s + 1)
                if later(i) or s:
                    act.wait_ge(s_look, b)
                for a, e in ((0, min(n, 8)), (8, n)):
                    if a < e:
                        ins = nc.scalar.copy(low_t[:, a:e, :].rearrange("p k q -> p (k q)"),
                                             flip[:, a // 8, 0:(e - a) * P])
                ins.then_inc(s_low, 1)
                for k in range(n):
                    act.wait_ge(s_table, b + k + 1)
                    if later(i) or s or k >= 2:
                        act.wait_ge(s_look, b + k - 1)
                    nc.scalar.copy(count[:, (s * K + k) % 2, :], table[:, 0:NT]).then_inc(s_count, 1)
            run(act, body)

        @block.vector
        def _(dve):
            def body(i, s, n):
                b = 2 * K * i + s * K
                dve.tensor_copy(src[:, s, 0:n], g.src[:, bass.ds(b, n)]).then_inc(s_src, 1)
                if later(i):
                    dve.wait_ge(s_table, b - K + 1)
                for digit, to, m in ((g.src_lo, low, P), (g.src_hi, high, NT)):
                    dve.tensor_tensor(to[:, s, 0:n, :], digit[:, bass.ds(b, n)].unsqueeze(2).to_broadcast([P, n, m]),
                                      g.rowb[:, 0:m].unsqueeze(1).to_broadcast([P, n, m]), ALU.is_equal).then_inc(s_hot, 1)
                dve.wait_ge(s_row[s], 16 * (i + 1))
                dve.wait_ge(s_src, 2 * i + s + 1)
                for k in range(n):
                    dve.scalar_tensor_tensor(out=waste[:, :], in0=row[:, s, k, :], scalar=src[:, s, k:k + 1],
                                             in1=g.after[:, :], op0=ALU.is_equal, op1=ALU.mult,
                                             accum_out=same[:, k:k + 1]).then_inc(s_same, 1)
                    dve.wait_ge(s_same, b + k + 1)
                dve.wait_ge(s_hot, 4 * i + 2 * s + 2)
                for k in range(n):
                    dve.wait_ge(s_look, b + k + 1)
                    dve.scalar_tensor_tensor(out=waste[:, 0:NT], in0=look[:, (s * K + k) % 2, 0:NT], scalar=1.0,
                                             in1=high[:, s, k, :], op0=ALU.mult, op1=ALU.mult,
                                             accum_out=before[:, k:k + 1]).then_inc(s_before, 1)
                    dve.wait_ge(s_before, b + k + 1)
                if later(i):
                    dve.wait_ge(s_scat[s], 16 * K * i)
                ins = dve.tensor_tensor(place[:, s, 0:n], same[:, 0:n], before[:, 0:n], ALU.add)
                if n == K:
                    ins.then_inc(s_place, 1)
                else:
                    ins.then_inc(s_sum, 1)
                    dve.wait_ge(s_sum, 1)
                    dve.tensor_copy(place[LONG:P, s, 0:1], g.trash[LONG:P, :]).then_inc(s_place, 1)
            run(dve, body)

        @block.tensor
        def _(pe):
            pe.matmul(table[:, 0:NT], g.ident[:, :], g.src_start[:, :], start=True, stop=False,
                      skip_group_check=True).then_inc(s_table, 1)

            def body(i, s, n):
                b = 2 * K * i + s * K
                pe.wait_ge(s_hot, 4 * i + 2 * s + 2)
                if later(i) or s:
                    pe.wait_ge(s_low, 2 * i + s)
                for k in range(n):
                    ins = pe.transpose(flip[:, k // 8, (k % 8) * P:(k % 8 + 1) * P], low[:, s, k, :], g.identb[:, :])
                ins.then_inc(s_flip, 1)
                pe.wait_ge(s_low, 2 * i + s + 1)
                for k in range(n):
                    pe.wait_ge(s_count, b + k + 1)
                    pe.matmul(table[:, 0:NT], low[:, s, k, :], high[:, s, k, :], start=False, stop=False,
                              skip_group_check=True).then_inc(s_table, 1)
                    if later(i) or s or k >= 2:
                        pe.wait_ge(s_before, b + k - 1)
                    pe.matmul(look[:, (s * K + k) % 2, 0:NT], low_t[:, k, :], count[:, (s * K + k) % 2, :],
                              start=True, stop=True).then_inc(s_look, 1)
            run(pe, body)


def terms_phase(nc, top, g, dram):
    with top.phase() as c, nc.Block() as block:
        s_clean = c.sem("te_scores_zeroed")
        data = c.sb("te_data", [P, 2, KN, HEADS])
        row = c.sb("te_row", [P, 2, KN], I32)
        first = c.sb("te_first", [P, 1], I32)
        head = c.sb("te_head", [P, HEADS])
        s_node = c.sem("te_node_terms_written")
        s_stage = c.sem("te_staged")
        s_first = c.sem("te_first_staged")
        s_go = c.sem("te_scatter_go")
        s_scat = [c.soft(f"te_scattered{s}") for s in range(2)]
        s_head = c.soft("te_head_gathered")
        s_load = c.sem("te_loaded")
        s_set = c.sem("te_heads_set")
        s_v = c.sem("te_vector_line")
        s_done = c.sem("te_scatter_done")

        @block.sync
        def _(sp):
            sp.dma_start(nodes(dram.node_terms), g.node_terms[:, :, :]).then_inc(s_node, 16)
            sp.wait_ge(s_done, 1)
            sp.wait_ge(s_clean, 1)
            long, short = chunked(dram.dst_terms[0:E])
            sp.dma_start(g.sdst[0:LONG, 0:STEPS + 1, :], long).then_inc(s_load, 16)
            sp.dma_start(g.sdst[LONG:P, 0:STEPS, :], short).then_inc(s_load, 16)

        @block.scalar
        def _(act):
            def body(i, s):
                if not isinstance(i, int):
                    act.wait_ge(s_scat[s], 16 * KN * i)
                nc.scalar.copy(data[:, s, :, :], g.node_terms[:, bass.ds(2 * KN * i + s * KN, KN), :])
                nc.scalar.copy(row[:, s, :], g.term_row[:, bass.ds(2 * KN * i + s * KN, KN)]).then_inc(s_stage, 1)
            nc.scalar.copy(first[:, :], g.dst_seg.first[:, :]).then_inc(s_first, 1)
            batches(act, NNB, body)

        @block.gpsimd
        def _(pool):
            pool.wait_ge(s_node, 16)
            pool.wait_ge(s_first, 1)
            pool.indirect_dma_start(out=head[:, :], out_offset=None, in_=dram.node_terms[:, :],
                                    in_offset=bass.IndirectOffsetOnAxis(ap=first[:, :], axis=0)).then_inc(s_head, 16)

            def body(i, s):
                pool.wait_ge(s_stage, 2 * i + s + 1)
                pool.sem_inc(s_go, 1)
                for k in range(KN):
                    pool.indirect_dma_start(
                        out=dram.dst_terms[:, :], in_=data[:, s, k, :], in_offset=None,
                        out_offset=bass.IndirectOffsetOnAxis(ap=row[:, s, k:k + 1], axis=0)).then_inc(s_scat[s], 16)
                    pool.wait_ge(s_scat[s], 16 * KN * i + 16 * (k + 1))
                    pool.sem_inc(s_go, 1)
            batches(pool, NNB, body)
            pool.sem_inc(s_done, 1)

        @block.vector
        def _(dve):
            dve.memset(g.sdst[:, STEPS, :], 0.0).then_inc(s_clean, 1)
            dve.wait_ge(s_head, 16)
            dve.wait_ge(s_load, 32)
            dve.tensor_copy(g.sdst[:, 0, :], head[:, :]).then_inc(s_set, 1)
            dve.wait_ge(s_set, 1)
            line = Line(dve, s_v)
            for h in range(HEADS):
                line(dve.tensor_tensor_scan(g.sdst[:, 0:STEPS + 1, h], g.keep[:, 0:STEPS + 1], g.sdst[:, 0:STEPS + 1, h],
                                            0.0, ALU.mult, ALU.add))


def reload_phase(nc, top, g, dram):
    with top.phase() as c, nc.Block() as block:
        s_load = c.sem("re_loaded")
        s_v = c.sem("re_vector_line")

        @block.sync
        def _(sp):
            long, short = chunked(dram.sorted[0:E])
            sp.dma_start(g.pay[0:LONG, 0:STEPS + 1, :], long).then_inc(s_load, 16)
            sp.dma_start(g.pay[LONG:P, 0:STEPS, :], short).then_inc(s_load, 16)

        @block.vector
        def _(dve):
            line = Line(dve, s_v)
            dve.wait_ge(s_load, 32)
            line(dve.tensor_scalar(g.src[:, :], g.pay[:, :, 1], (1 << RSHIFT) - 1, None, ALU.bitwise_and))
            line(dve.tensor_tensor(g.keep[:, 1:W], g.src[:, 1:W], g.src[:, 0:W - 1], ALU.is_equal))


def weight_phase(nc, top, g):
    with top.phase() as c, nc.Block() as block:
        T = STEPS + 1
        rel = c.sb("we_relation", [P, T])
        rel_i = c.sb("we_relation_bits", [P, T], I32)
        is_first = c.sb("we_in_first", [P, T])
        is_last = c.sb("we_in_last", [P, T])
        is_rel = c.sb("we_is_relation", [P, T])
        up = c.sb("we_count_up", [P, T])
        down = c.sb("we_count_down", [P, T])
        heads = c.sb("we_first_counts", [P, REL])
        tails = c.sb("we_last_counts", [P, REL])
        others = c.sb("we_other_chunks", [P, 2, REL])
        ps = c.ps("we_carried", [P, 2, REL])
        s_v = c.sem("we_vector_line")
        s_cnt = c.sem("we_counts_ready")
        s_ps = c.sem("we_carried_ready")
        seg = g.src_seg

        @block.vector
        def _(dve):
            line = Line(dve, s_v)
            line(dve.tensor_scalar(rel_i[:, :], g.pay[:, 0:T, 1], RSHIFT, None, ALU.logical_shift_right))
            line(dve.tensor_copy(rel[:, :], rel_i[:, :]))
            line(dve.memset(rel[LONG:P, STEPS:T], -1.0))
            line(dve.tensor_scalar(is_first[:, :], g.src[:, 0:T], seg.first[:, 0:1], None, ALU.is_equal))
            line(dve.tensor_scalar(is_last[:, :], g.src[:, 0:T], seg.last[:, 0:1], None, ALU.is_equal))
            for r in range(REL):
                line(dve.scalar_tensor_tensor(out=up[:, :], in0=rel[:, :], scalar=float(r), in1=is_first[:, :],
                                              op0=ALU.is_equal, op1=ALU.mult, accum_out=heads[:, r:r + 1]))
                line(dve.scalar_tensor_tensor(out=up[:, :], in0=rel[:, :], scalar=float(r), in1=is_last[:, :],
                                              op0=ALU.is_equal, op1=ALU.mult, accum_out=tails[:, r:r + 1]))
            dve.sem_inc(s_cnt, 1)
            dve.wait_ge(s_ps, 2)
            line(dve.tensor_copy(others[:, :, :], ps[:, :, :]))
            line(dve.memset(g.keep[:, 0:1], 1.0))
            line(dve.memset(g.keep[LONG:P, STEPS:STEPS + 1], 1.0))
            line(dve.memset(g.keep[:, STEPS + 1:STEPS + 2], 1.0))
            line(dve.memset(g.weight[:, :], 0.0))
            for r in range(REL):
                line(dve.tensor_scalar(is_rel[:, :], rel[:, :], float(r), None, ALU.is_equal))
                line(dve.tensor_tensor_scan(up[:, :], g.keep[:, 0:T], is_rel[:, :], others[:, 0, r:r + 1],
                                            ALU.mult, ALU.add))
                line(dve.tensor_tensor_scan(down[:, ::-1], g.keep[:, 1:T + 1][:, ::-1], is_rel[:, ::-1],
                                            others[:, 1, r:r + 1], ALU.mult, ALU.add))
                line(dve.scalar_tensor_tensor(out=up[:, :], in0=up[:, :], scalar=-1.0, in1=down[:, :],
                                              op0=ALU.add, op1=ALU.add))
                line(dve.tensor_tensor(up[:, :], up[:, :], is_rel[:, :], ALU.mult))
                line(dve.tensor_tensor(g.weight[:, 0:T], g.weight[:, 0:T], up[:, :], ALU.add))
            line(dve.tensor_scalar(g.weight[:, :], g.weight[:, :], 1.0, None, ALU.max))
            line(dve.reciprocal(g.weight[:, :], g.weight[:, :]))
            line(dve.memset(g.keep[:, 0:1], 0.0))

        @block.tensor
        def _(pe):
            pe.wait_ge(s_v, 5 + 2 * REL)
            pe.matmul(ps[:, 0, :], seg.carry_mask[:, :], tails[:, :], start=True, stop=True).then_inc(s_ps, 1)
            pe.matmul(ps[:, 1, :], seg.carry_mask_t[:, :], heads[:, :], start=True, stop=True).then_inc(s_ps, 1)


def carry_phase(nc, top, g, tag, rows, seg, attention=False):
    width = AW if attention else D
    with top.phase() as c, nc.Block() as block:
        index = c.sb(f"{tag}_index", [P, 1], I32)
        row = c.sb(f"{tag}_row", [P, width])
        new = c.sb(f"{tag}_new_row", [P, width])
        carried = c.ps(f"{tag}_carried", [P, 512])
        s_index = c.sem(f"{tag}_index_ready")
        s_row = c.soft(f"{tag}_row_gathered")
        s_sum = c.sem(f"{tag}_carried_summed")
        s_new = c.sem(f"{tag}_new_row_ready")
        s_out = c.soft(f"{tag}_row_written")
        if attention:
            diag = c.sb(f"{tag}_diag", [P, HEADS, P])
            open_t = c.sb(f"{tag}_open", [P, P])
            score = c.sb(f"{tag}_scores", [P, HEADS, P])
            share = c.sb(f"{tag}_shares", [P, HEADS, P])
            share_t = c.sb(f"{tag}_shares_transposed", [P, HEADS, P])
            m = c.sb(f"{tag}_max", [P, HEADS])
            own = c.sb(f"{tag}_own", [P, HEADS])
            spread = c.ps(f"{tag}_spread", [P, HEADS, P])
            flipped = c.ps(f"{tag}_flipped", [P, HEADS, P])
            s_v = c.sem(f"{tag}_vector_line")
            s_diag = c.sem(f"{tag}_diagonals")
            s_spread = c.sem(f"{tag}_max_spread")
            s_score = c.sem(f"{tag}_exponents_ready")
            s_share = c.sem(f"{tag}_shares_ready")
            s_flip = c.sem(f"{tag}_shares_flipped")
            s_st = c.sem(f"{tag}_shares_copied")
            tail = g.tail[:, :].rearrange("p (h w) -> p h w", h=HEADS)
            row_h = row[:, :].rearrange("p (h w) -> p h w", h=HEADS)
            new_h = new[:, :].rearrange("p (h w) -> p h w", h=HEADS)

        @block.gpsimd
        def _(pool):
            pool.wait_ge(s_index, 1)
            pool.indirect_dma_start(out=row[:, :], out_offset=None, in_=rows,
                                    in_offset=bass.IndirectOffsetOnAxis(ap=index[:, :], axis=0)).then_inc(s_row, 16)
            pool.wait_ge(s_new, 1)
            pool.indirect_dma_start(out=rows, in_=new[:, :], in_offset=None,
                                    out_offset=bass.IndirectOffsetOnAxis(ap=index[:, :], axis=0)).then_inc(s_out, 16)
            pool.wait_ge(s_out, 16)

        @block.vector
        def _(dve):
            dve.tensor_copy(index[:, :], seg.first_end[:, :]).then_inc(s_index, 1)
            if not attention:
                dve.wait_ge(s_row, 16)
                dve.wait_ge(s_sum, 1)
                dve.tensor_tensor(new[:, :], row[:, :], carried[:, 0:D], ALU.add).then_inc(s_new, 1)
                return
            line = Line(dve, s_v)
            for h in range(HEADS):
                ins = dve.tensor_scalar(diag[:, h, :], g.ident[:, :], tail[:, h, HD + 1:HD + 2], None, ALU.mult)
            ins.then_inc(s_diag, 1)
            line(dve.tensor_scalar(open_t[:, :], seg.carry_mask_t[:, :], -1.0, FAR, ALU.add, ALU.mult))
            dve.wait_ge(s_spread, 1)
            line(dve.tensor_tensor(score[:, :, :], spread[:, :, :],
                                   open_t[:, :].unsqueeze(1).to_broadcast([P, HEADS, P]), ALU.add))
            line(dve.tensor_reduce(m[:, :], score[:, :, :], AX.X, ALU.max))
            dve.wait_ge(s_row, 16)
            line(dve.tensor_tensor(m[:, :], m[:, :], row_h[:, :, HD + 1], ALU.max))
            line(dve.tensor_tensor(own[:, :], row_h[:, :, HD + 1], m[:, :], ALU.subtract))
            dve.tensor_tensor(score[:, :, :], score[:, :, :], m[:, :].unsqueeze(2).to_broadcast([P, HEADS, P]),
                              ALU.subtract).then_inc(s_score, 1)
            dve.wait_ge(s_flip, 1)
            dve.tensor_copy(share_t[:, :, :], flipped[:, :, :]).then_inc(s_st, 1)
            dve.wait_ge(s_sum, 1)
            dve.wait_ge(s_share, 2)
            line(dve.tensor_copy(new[:, :], row[:, :]))
            line(dve.tensor_tensor(new_h[:, :, 0:HD + 1], row_h[:, :, 0:HD + 1],
                                   own[:, :].unsqueeze(2).to_broadcast([P, HEADS, HD + 1]), ALU.mult))
            dve.tensor_tensor(new_h[:, :, 0:HD + 1], new_h[:, :, 0:HD + 1],
                              carried[:, 0:HEADS * (HD + 1)].rearrange("p (h w) -> p h w", h=HEADS),
                              ALU.add).then_inc(s_new, 1)

        @block.scalar
        def _(act):
            if attention:
                act.wait_ge(s_score, 1)
                nc.scalar.activation(share[:, :, :], score[:, :, :], ACT.Exp).then_inc(s_share, 1)
                nc.scalar.activation(own[:, :], own[:, :], ACT.Exp).then_inc(s_share, 1)

        @block.tensor
        def _(pe):
            if not attention:
                pe.matmul(carried[:, 0:D], seg.carry_mask[:, :], g.tail[:, 0:D], start=True, stop=True).then_inc(s_sum, 1)
                return
            pe.wait_ge(s_diag, 1)
            pe.matmul(spread[:, :, :].rearrange("p h q -> p (h q)"), g.ones[:, :],
                      diag[:, :, :].rearrange("p h q -> p (h q)"), start=True, stop=True).then_inc(s_spread, 1)
            pe.wait_ge(s_share, 1)
            for h in range(HEADS):
                ins = pe.transpose(flipped[:, h, :], share[:, h, :], g.ident[:, :])
            ins.then_inc(s_flip, 1)
            pe.wait_ge(s_st, 1)
            for h in range(HEADS):
                ins = pe.matmul(carried[:, h * (HD + 1):(h + 1) * (HD + 1)], share_t[:, h, :], tail[:, h, 0:HD + 1],
                                start=True, stop=True)
            ins.then_inc(s_sum, 1)


def update_phase(nc, top, g, layer, rows, last, has, dram):
    tag = f"u{layer}"
    width = AW if layer == 2 else D
    with top.phase() as c, nc.Block() as block:
        index = c.sb(f"{tag}_index", [P, 2, KN], I32)
        got = c.sb(f"{tag}_gathered", [P, 2, KN, width])
        near = c.sb(f"{tag}_neighbours", [P, KN, D])
        s_index = c.sem(f"{tag}_index_staged")
        s_got = [c.soft(f"{tag}_gathered{s}") for s in range(2)]
        s_go = c.sem(f"{tag}_gather_go")
        s_used = c.sem(f"{tag}_gathered_used")
        s_add = c.sem(f"{tag}_added")
        s_st = c.sem(f"{tag}_stats")
        s_root = c.sem(f"{tag}_root")
        s_n = c.sem(f"{tag}_norm_line")
        s_h = c.sem(f"{tag}_h_ready")
        s_in = c.sem(f"{tag}_inputs_ready")
        s_t = c.sem(f"{tag}_transposed")
        s_tc = c.sem(f"{tag}_transposes_copied")
        s_m = c.sem(f"{tag}_products_ready")
        s_v = c.sem(f"{tag}_vector_line")
        s_z = c.sem(f"{tag}_hidden_ready")
        s_zb = c.sem(f"{tag}_hidden_biased")
        s_zl = c.sem(f"{tag}_hidden_activated")
        s_out = c.sem(f"{tag}_x_out")
        flat = lambda ap: ap.rearrange("p k d -> p (k d)")
        if layer < 2:
            h = c.sb(f"{tag}_h", [P, KN, D])
            ins_t = c.sb(f"{tag}_inputs_transposed", [P, 2, KN * D])
            hid = c.sb(f"{tag}_hidden", [P, KN * D])
            hid_a = c.sb(f"{tag}_hidden_act", [P, KN * D])
            tp = c.ps(f"{tag}_transposes", [P, 2, 1024])
            mm = c.ps(f"{tag}_products", [P, 1024])
            zz = c.ps(f"{tag}_hidden_products", [P, 1024])
        if layer == 2:
            den = c.sb(f"{tag}_denominator", [P, KN, HEADS])
            neg = c.sb(f"{tag}_negative_part", [P, KN * D])
        later = lambda i: not isinstance(i, int) or i > 0
        at = lambda i, s: 2 * i + s

        @block.gpsimd
        def _(pool):
            def body(i, s):
                pool.wait_ge(s_index, at(i, s) + 1)
                if later(i):
                    pool.wait_ge(s_used, at(i, s) - 1)
                pool.sem_inc(s_go, 1)
                for k in range(KN):
                    pool.indirect_dma_start(
                        out=got[:, s, k, :], out_offset=None, in_=rows,
                        in_offset=bass.IndirectOffsetOnAxis(ap=index[:, s, k:k + 1], axis=0)).then_inc(s_got[s], 16)
            batches(pool, NNB, body)

        @block.scalar
        def _(act):
            def stage(i, s):
                nc.scalar.copy(index[:, s, :], last[:, bass.ds(KN * (2 * i + s), KN)]).then_inc(s_index, 1)

            def body(i, s):
                if later(i):
                    act.wait_ge(s_got[s], 16 * KN * i)
                stage(i, s)
                if layer < 2:
                    if later(i) or s:
                        act.wait_ge(s_in if layer else s_t, at(i, s))
                    for k in range(KN):
                        j = 2 * KN * i + s * KN + k
                        nc.scalar.activation(h[:, k:k + 1, :], g.x[:, bass.ds(j, 1), :], ACT.Relu,
                                             bias=g.shift[:, bass.ds(j, 1)], scale=g.scale[:, bass.ds(j, 1)]).then_inc(s_h, 1)
                if layer == 1:
                    act.wait_ge(s_z, at(i, s) + 1)
                    for a, b in GN:
                        ins = nc.scalar.activation(hid[:, a * D:b * D], zz[:, a * D:b * D], ACT.Identity, bias=g.b1[:, 0:1])
                    ins.then_inc(s_zb, 1)
                if layer == 2:
                    act.wait_ge(s_in, at(i, s) + 1)
                    nc.scalar.activation(neg[:, :], neg[:, :], ACT.Exp).then_inc(s_zb, 1)
            batches(act, NNB, body)
            if layer < 3:
                act.wait_ge(s_n, 6)
                nc.scalar.activation(g.shift[:, :], g.scale[:, :], ACT.Sqrt).then_inc(s_root, 1)

        @block.vector
        def _(dve):
            line = Line(dve, s_v)
            links = (1, 2, 5, 1)[layer]

            def body(i, s):
                line.at(links * at(i, s))
                b = 2 * KN * i + s * KN
                x = g.x[:, bass.ds(b, KN), :]
                dve.wait_ge(s_got[s], 16 * KN * (i + 1))
                if layer == 0 and (later(i) or s):
                    dve.wait_ge(s_t, at(i, s))
                if layer == 3 and (later(i) or s):
                    dve.wait_ge(s_add, at(i, s))
                has_b = has[:, bass.ds(b, KN)].unsqueeze(2)
                if layer != 2:
                    dve.tensor_tensor(near[:, :, :], got[:, s, :, :], has_b.to_broadcast([P, KN, D]),
                                      ALU.mult).then_inc(s_used, 1)
                    dve.wait_ge(s_used, at(i, s) + 1)
                if layer < 2:
                    if layer == 1:
                        dve.wait_ge(s_h, KN * (at(i, s) + 1))
                        if later(i) or s:
                            dve.wait_ge(s_t, at(i, s))
                        dve.scalar_tensor_tensor(out=near[:, :, :], in0=h[:, :, :], scalar=2.0, in1=near[:, :, :],
                                                 op0=ALU.mult, op1=ALU.add).then_inc(s_in, 1)
                    dve.wait_ge(s_t, at(i, s) + 1)
                    ins = dve.tensor_copy(ins_t[:, 0, :], tp[:, 0, 0:KN * D])
                    if layer == 0:
                        ins = dve.tensor_copy(ins_t[:, 1, :], tp[:, 1, 0:KN * D])
                    ins.then_inc(s_tc, 1)
                    if layer == 1:
                        dve.wait_ge(s_zb, at(i, s) + 1)
                        dve.scalar_tensor_tensor(out=hid_a[:, :], in0=hid[:, :], scalar=0.01, in1=hid[:, :],
                                                 op0=ALU.mult, op1=ALU.max).then_inc(s_zl, 1)
                    dve.wait_ge(s_m, at(i, s) + 1)
                    if layer == 0:
                        dve.scalar_tensor_tensor(out=flat(x), in0=mm[:, 0:KN * D], scalar=0.0, in1=flat(x),
                                                 op0=ALU.max, op1=ALU.add).then_inc(s_add, 1)
                    else:
                        dve.tensor_tensor(flat(x), mm[:, 0:KN * D], flat(x), ALU.add).then_inc(s_add, 1)
                elif layer == 2:
                    r = got[:, s, :, :].rearrange("p k (h w) -> p k h w", h=HEADS)
                    line(dve.tensor_scalar(den[:, :, :], r[:, :, :, HD], 1e-8, None, ALU.add))
                    line(dve.reciprocal(den[:, :, :], den[:, :, :]))
                    line(dve.tensor_tensor(den[:, :, :], den[:, :, :], has_b.to_broadcast([P, KN, HEADS]), ALU.mult))
                    dve.tensor_tensor(near[:, :, :].rearrange("p k (h w) -> p (k h) w", h=HEADS),
                                      r[:, :, :, 0:HD].rearrange("p k h w -> p (k h) w"),
                                      den[:, :, :].rearrange("p k h -> p (k h)").unsqueeze(2)
                                      .to_broadcast([P, KN * HEADS, HD]), ALU.mult).then_inc(s_used, 1)
                    dve.wait_ge(s_used, at(i, s) + 1)
                    dve.tensor_scalar(neg[:, :], flat(near[:, :, :]), 0.0, None, ALU.min).then_inc(s_in, 1)
                    line(dve.tensor_scalar(flat(near[:, :, :]), flat(near[:, :, :]), 0.0, -1.0, ALU.max, ALU.add))
                    dve.wait_ge(s_zb, at(i, s) + 1)
                    line(dve.tensor_tensor(flat(near[:, :, :]), flat(near[:, :, :]), neg[:, :], ALU.add))
                    dve.tensor_tensor(flat(x), flat(x), flat(near[:, :, :]), ALU.add).then_inc(s_add, 1)
                else:
                    dve.scalar_tensor_tensor(out=flat(x), in0=flat(near[:, :, :]), scalar=0.0, in1=flat(x),
                                             op0=ALU.max, op1=ALU.add).then_inc(s_add, 1)
                if layer < 3:
                    dve.wait_ge(s_add, at(i, s) + 1)
                    for k in range(KN):
                        ins = dve.bn_stats(g.stats[:, bass.ds(b + k, 1), :], g.x[:, bass.ds(b + k, 1), :])
                    ins.then_inc(s_st, 1)
            batches(dve, NNB, body)
            if layer < 3:
                dve.wait_ge(s_st, NNB)
                norm_stats(Line(dve, s_n), lambda: dve.wait_ge(s_root, 1), g)

        @block.tensor
        def _(pe):
            if layer >= 2:
                return

            def body(i, s):
                if later(i) or s:
                    pe.wait_ge(s_tc, at(i, s))
                if layer == 0:
                    pe.wait_ge(s_h, KN * (at(i, s) + 1))
                    pe.wait_ge(s_used, at(i, s) + 1)
                else:
                    pe.wait_ge(s_in, at(i, s) + 1)
                for k in range(KN):
                    if layer == 0:
                        pe.transpose(tp[:, 1, k * D:(k + 1) * D], h[:, k, :], g.ident[:, :])
                    ins = pe.transpose(tp[:, 0, k * D:(k + 1) * D], near[:, k, :], g.ident[:, :])
                ins.then_inc(s_t, 1)
                pe.wait_ge(s_tc, at(i, s) + 1)
                if layer == 1:
                    if later(i) or s:
                        pe.wait_ge(s_zb, at(i, s))
                    for a, b in GN:
                        ins = pe.matmul(zz[:, a * D:b * D], g.w1[:, :], ins_t[:, 0, a * D:b * D], start=True, stop=True)
                    ins.then_inc(s_z, 1)
                    pe.wait_ge(s_zl, at(i, s) + 1)
                if later(i) or s:
                    pe.wait_ge(s_add, at(i, s))
                for k in range(KN):
                    to = mm[:, k * D:(k + 1) * D]
                    part = slice(k * D, (k + 1) * D)
                    if layer == 0:
                        pe.matmul(to, ins_t[:, 1, part], g.w0_h[:, :], start=True, stop=False)
                        pe.matmul(to, ins_t[:, 0, part], g.w0_near[:, :], start=False, stop=False)
                        ins = pe.matmul(to, g.ones[0:1, :], g.b0_apply[0:1, :], start=False, stop=True)
                    else:
                        pe.matmul(to, hid_a[:, part], g.w2[:, :], start=True, stop=False)
                        ins = pe.matmul(to, g.ones[0:1, :], g.b2[0:1, :], start=False, stop=True)
                ins.then_inc(s_m, 1)
            batches(pe, NNB, body)

        @block.sync
        def _(sp):
            if layer == 3:
                sp.wait_ge(s_add, NNB)
                sp.dma_start(nodes(dram.out[0:(NT - 1) * P, :]), g.x[:, 0:NT - 1, :]).then_inc(s_out, 16)
                sp.dma_start(dram.out[(NT - 1) * P:N, :], g.x[0:TAIL, NT - 1, :]).then_inc(s_out, 16)
                sp.wait_ge(s_out, 32)


def weights_phase(nc, top, g, dram):
    with top.phase() as c, nc.Block() as block:
        w = c.sb("wt_w", [P, D])
        a = c.sb("wt_a", [P, 2 * HEADS])
        ps = c.ps("wt_scores", [P, 2 * HEADS])
        s_zero = c.sem("wt_zeroed")
        s_load = c.sem("wt_loaded")
        s_a = c.sem("wt_attention_loaded")
        s_m = c.sem("wt_scores_ready")
        s_done = c.sem("wt_done")
        pairs = [(g.w0_edge[:, :], dram.w0_edge), (g.w0_node[:, :], dram.w0_node), (g.b0_msg[:, :], dram.b0_msg),
                 (g.w0_h[:, :], dram.w0_h), (g.w0_near[:, :], dram.w0_near), (g.b0_apply[:, :], dram.b0_apply),
                 (g.w1[:, :], dram.w1), (g.b1[:, :], dram.b1), (g.w2[:, :], dram.w2), (g.b2[:, :], dram.b2),
                 (g.wx[:, 0:D], dram.w_att_t), (w[:, :], dram.w_att), (g.w3[:, :], dram.w3)]

        @block.gpsimd
        def _(pool):
            pool.memset(a[:, :], 0.0).then_inc(s_zero, 1)

        @block.sync
        def _(sp):
            for to, src in pairs:
                sp.dma_start(to, src).then_inc(s_load, 16)
            sp.wait_ge(s_zero, 1)
            for h in range(HEADS):
                for n in range(2):
                    sp.dma_start(a[h * HD:(h + 1) * HD, n * HEADS + h:n * HEADS + h + 1],
                                 dram.a_w[n * HD:(n + 1) * HD, :]).then_inc(s_a, 16)
            sp.wait_ge(s_load, 16 * len(pairs))

        @block.tensor
        def _(pe):
            pe.wait_ge(s_load, 16 * len(pairs))
            pe.wait_ge(s_a, 16 * 2 * HEADS)
            pe.matmul(ps[:, :], w[:, :], a[:, :], start=True, stop=True).then_inc(s_m, 1)

        @block.vector
        def _(dve):
            dve.wait_ge(s_m, 1)
            dve.tensor_copy(g.wx[:, D:D + 2 * HEADS], ps[:, :]).then_inc(s_done, 1)


class Names:
    pass


def segments(top, tag):
    seg = Names()
    seg.first, seg.last, seg.first_end = (top.sb(f"{tag}_{n}", [P, 1]) for n in ("first", "last", "first_end"))
    seg.carry_mask, seg.carry_mask_t = (top.sb(f"{tag}_{n}", [P, P]) for n in ("carry_mask", "carry_mask_t"))
    return seg


def build(nc, dram):
    with ExitStack() as ctx:
        top = Core(nc, ctx)
        top.shared = ctx
        g = Names()
        g.x = top.sb("x", [P, NT, D])
        g.src, g.dst = top.sb("src", [P, W], I32), top.sb("dst", [P, W], I32)
        g.pay = top.sb("payload", [P, W, 2], I32)
        g.keep = top.sb("keep", [P, W])
        turns = top.sb("edge_turns", [P, (STEPS + 1) * HEADS])
        g.src_lo, g.src_hi, g.dst_lo, g.dst_hi = (turns[:, n * W // 2:(n + 1) * W // 2].bitcast(BF16) for n in range(4))
        g.sdst = turns[:, :].rearrange("p (t h) -> p t h", h=HEADS)
        g.weight = turns[:, 0:W]
        g.stats = top.sb("stats", [P, NT, 6])
        g.mean, g.scale, g.shift = (top.sb(n, [P, NT]) for n in ("mean_sum", "norm_scale", "norm_shift"))
        g.ident, g.ones, g.before, g.upto, g.after, g.row = (
            top.sb(n, [P, P]) for n in ("ident", "ones", "before", "upto", "after", "row_numbers"))
        g.identb, g.rowb = top.sb("ident_bf16", [P, P], BF16), top.sb("row_numbers_bf16", [P, P], BF16)
        g.part, g.chunk_start = top.sb("partition_number", [P, 1]), top.sb("chunk_start", [P, 1])
        g.trash = top.sb("trash_row", [P, 1], I32)
        g.tail = top.sb("chunk_ends", [P, AW])
        g.src_hist, g.dst_hist, g.src_start, g.dst_start, g.src_has, g.dst_has = (
            top.sb(n, [P, NT]) for n in ("src_hist", "dst_hist", "src_start", "dst_start", "src_has", "dst_has"))
        g.src_last, g.dst_last, g.term_row = (top.sb(n, [P, NT], I32) for n in ("src_last", "dst_last", "term_row"))
        g.node_terms = top.sb("node_terms", [P, NT, HEADS])
        g.w0_edge = top.sb("w0_edge", [DE, D])
        g.w0_node, g.w0_h, g.w0_near, g.w1, g.w2 = (top.sb(n, [P, D]) for n in ("w0_node", "w0_h", "w0_near", "w1", "w2"))
        g.b0_msg, g.b0_apply, g.b2 = (top.sb(n, [1, D]) for n in ("b0_msg", "b0_apply", "b2"))
        g.b1 = top.sb("b1", [P, 1])
        g.wx = top.sb("wx", [P, D + 2 * HEADS])
        g.w3 = top.sb("w3", [P, REL * D])
        g.dst_seg, g.src_seg = segments(top, "dst_segments"), segments(top, "src_segments")

        scratch = lambda n, shape, dt=F32: nc.dram_tensor(n, shape, dt).ap()
        dram.table0 = scratch("node_table", [NPAD, D])
        dram.table2 = scratch("attention_table", [NPAD, AW])
        dram.table3 = scratch("relation_table", [REL * NPAD, D])
        dram.rows = scratch("segment_rows", [E, D])
        dram.rows2 = scratch("attention_rows", [E, AW])
        dram.sorted = scratch("sorted_edges", [E + P, 2], I32)
        dram.dst_terms = scratch("dst_terms", [E + P, HEADS])
        dram.node_terms = scratch("node_terms_rows", [NPAD, HEADS])

        setup_phase(nc, top, g, dram)
        weights_phase(nc, top, g, dram)
        boundary_phase(nc, top, g, "bd", g.dst, None, g.dst_seg)
        first_norm_phase(nc, top, g)
        by_column = lambda table: lambda j, k: nodes(table)[:, bass.ds(j, k), :]
        project_phase(nc, top, g, "p0", by_column(dram.table0), g.w0_node, D, g.b0_msg, D,
                      copy_act=lambda to, ps: nc.scalar.copy(to, ps[:, 0:D]))
        edge_phase_0(nc, top, g, dram)
        order_phase(nc, top, g)
        sort_phase(nc, top, g, dram)
        carry_phase(nc, top, g, "c0", dram.rows[:, :], g.dst_seg)
        update_phase(nc, top, g, 0, dram.rows[:, :], g.dst_last, g.dst_has, dram)
        project_phase(nc, top, g, "p1", by_column(dram.table0))
        edge_phase_1(nc, top, g, dram)
        carry_phase(nc, top, g, "c1", dram.rows[:, :], g.dst_seg)
        update_phase(nc, top, g, 1, dram.rows[:, :], g.dst_last, g.dst_has, dram)

        heads = lambda ap: ap.rearrange("p (h w) -> p h w", h=HEADS)

        def ones_column(dve, out, ready):
            dve.memset(out[:, :, :, :].rearrange("p s k (h w) -> p (s k h) w", h=HEADS)[:, :, HD], 1.0).then_inc(ready, 1)

        def scores(to, ps, j):
            nc.vector.tensor_copy(g.node_terms[:, bass.ds(j, 1), :], ps[:, 512 + HEADS:512 + 2 * HEADS].unsqueeze(1))
            return nc.vector.tensor_copy(heads(to)[:, :, HD + 1], ps[:, 512:512 + HEADS])
        project_phase(nc, top, g, "p2", by_column(dram.table2), g.wx, D + 2 * HEADS, None, AW,
                      copy_act=lambda to, ps: nc.scalar.copy(heads(to)[:, :, 0:HD], heads(ps[:, 0:D])),
                      copy_dve=scores, prepare=ones_column)
        terms_phase(nc, top, g, dram)
        edge_phase_2(nc, top, g, dram)
        carry_phase(nc, top, g, "c2", dram.rows2[:, :], g.dst_seg, attention=True)
        update_phase(nc, top, g, 2, dram.rows2[:, :], g.dst_last, g.dst_has, dram)

        by_relation = lambda j, k: dram.table3.rearrange("(r j p) d -> p r j d", r=REL, p=P)[:, :, bass.ds(j, 1), :].rearrange(
            "p r j d -> p r (j d)")
        project_phase(nc, top, g, "p3", by_relation, g.w3, REL * D, None, REL * D,
                      copy_act=lambda to, ps: nc.scalar.copy(to[:, 0:512], ps[:, 0:512]),
                      copy_dve=lambda to, ps, j: nc.vector.tensor_copy(to[:, 512:1024], ps[:, 512:1024]), writes=KN)
        reload_phase(nc, top, g, dram)
        boundary_phase(nc, top, g, "bs", g.src, None, g.src_seg)
        weight_phase(nc, top, g)
        edge_phase_3(nc, top, g, dram)
        carry_phase(nc, top, g, "c3", dram.rows[:, :], g.src_seg)
        update_phase(nc, top, g, 3, dram.rows[:, :], g.src_last, g.src_has, dram)


def kernel(x, src, dst, edge_attr_128, edge_attr_64, edge_type_8, L0_gnn_W_msg_w, L0_gnn_W_msg_b, L0_gnn_W_apply_w,
           L0_gnn_W_apply_b, L1_gnn_W1, L1_gnn_b1, L1_gnn_W2, L1_gnn_b2, L2_gnn_W, L2_gnn_a_w, L3_gnn_weights):
    import numpy as np
    import concourse.bacc as bacc
    from concourse.bass_utils import run_bass_kernel_spmd

    cut = LONG * (STEPS + 1)

    def by_step(a):
        out = np.zeros((P, STEPS + 1) + a.shape[1:], a.dtype)
        out[:LONG] = a[:cut].reshape((LONG, STEPS + 1) + a.shape[1:])
        out[LONG:, :STEPS] = a[cut:].reshape((P - LONG, STEPS) + a.shape[1:])
        return out.transpose(2, 1, 0)

    arr = lambda a: np.asarray(a)
    src_a = arr(src)
    w_msg, w_app, w_rel = arr(L0_gnn_W_msg_w), arr(L0_gnn_W_apply_w), arr(L3_gnn_weights)
    given = {
        "x": arr(x), "src": src_a, "dst": arr(dst), "edge_type_8": arr(edge_type_8),
        "edge_attr_128": arr(edge_attr_128), "edge64_t": by_step(arr(edge_attr_64)),
        "src_t": by_step(src_a[:, None])[0],
        "w0_node": w_msg[:, :D].T, "w0_edge": w_msg[:, D:].T, "b0_msg": arr(L0_gnn_W_msg_b)[None, :],
        "w0_h": w_app[:, :D].T, "w0_near": w_app[:, D:].T, "b0_apply": arr(L0_gnn_W_apply_b)[None, :],
        "w1": arr(L1_gnn_W1), "b1": arr(L1_gnn_b1)[:, None], "w2": arr(L1_gnn_W2), "b2": arr(L1_gnn_b2)[None, :],
        "w_att": arr(L2_gnn_W), "w_att_t": arr(L2_gnn_W).T, "a_w": arr(L2_gnn_a_w)[:, None],
        "w3": w_rel.transpose(2, 0, 1).reshape(D, REL * D),
    }
    nc = bacc.Bacc("TRN2", target_bir_lowering=False, num_devices=1)
    dram, arrays = Names(), {}
    for name, a in given.items():
        a = np.ascontiguousarray(a)
        arrays[f"in_{name}"] = a
        ap = nc.dram_tensor(f"in_{name}", a.shape, mybir.dt.from_np(a.dtype), kind="ExternalInput").ap()
        dram.__dict__[name] = ap
    dram.out = nc.dram_tensor("out_x", (N, D), F32, kind="ExternalOutput").ap()
    build(nc, dram)
    r = run_bass_kernel_spmd(nc, [arrays], core_ids=[0])
    return r.results[0]["out_x"]
```

```python
from contextlib import ExitStack

import concourse.bass as bass
from concourse import mybir

F32 = mybir.dt.float32
BF16 = mybir.dt.bfloat16
I32 = mybir.dt.int32
ALU = mybir.AluOpType
ACT = mybir.ActivationFunctionType
AX = mybir.AxisListType

P = 128
N, E, D, DE = 12500, 200000, 128, 64
HEADS, HD, REL = 4, 32, 8
NT = -(-N // P)
TAIL = N - (NT - 1) * P
NPAD = NT * P
STEPS = E // P
LONG = E - STEPS * P
K = 11
NB = STEPS // K
W = (NB + 2) * K
KN = 7
NNB = NT // KN
assert NB * K == STEPS and NB % 2 == 0 and NNB * KN == NT and NNB % 2 == 0
HW = HD + 2
AW = HEADS * HW
RSHIFT = 14
assert N <= 1 << RSHIFT
FAR = 1e30
SLOPE = 0.2
EPS = 1e-5
XP = 4
GK = [(g, min(g + 4, K)) for g in range(0, K, 4)]
GN = [(g, min(g + 4, KN)) for g in range(0, KN, 4)]


def batches(eng, count, body):
    body(0, 0)
    body(0, 1)
    with eng.Fori(1, count // 2) as i:
        body(i, 0)
        body(i, 1)


def lagged(eng, count, stages, last=None):
    def body(i, s):
        for stage, lag in stages:
            back = (s - lag) // 2
            if not isinstance(i, int) or i + back >= 0:
                stage(i + back if back else i, (s - lag) % 2)
    for i in range(2):
        body(i, 0)
        body(i, 1)
    with eng.Fori(2, count // 2) as i:
        body(i, 0)
        body(i, 1)
    if last is None:
        for late in range(max(lag for _, lag in stages)):
            for stage, lag in stages:
                if lag > late:
                    b = count + late - lag
                    stage(b // 2, b % 2)
    else:
        last()


class Line:

    def __init__(self, eng, sem):
        self.eng, self.sem, self.base, self.n = eng, sem, 0, 0

    def at(self, base):
        self.base, self.n = base, 0

    def __call__(self, ins):
        ins.then_inc(self.sem, 1)
        self.n += 1
        self.eng.wait_ge(self.sem, self.base + self.n)


def chunked(rows):
    cut = LONG * (STEPS + 1)
    return (rows[0:cut].rearrange("(p t) r -> p t r", t=STEPS + 1),
            rows[cut:E].rearrange("(p t) r -> p t r", t=STEPS))


def nodes(rows):
    return rows.rearrange("(j p) d -> p j d", p=P)


class Core:

    def __init__(self, nc, ctx, shared=None):
        self.nc, self.ctx, self.sems, self.shared = nc, ctx, [], shared

    def sem(self, name):
        self.sems.append(self.ctx.enter_context(self.nc.semaphore(name)))
        return self.sems[-1]

    def soft(self, name):
        return self.shared.enter_context(self.nc.semaphore(name))

    def sb(self, name, shape, dt=F32):
        return self.ctx.enter_context(self.nc.sbuf_tensor(name, shape, dt))

    def ps(self, name, shape, dt=F32):
        return self.ctx.enter_context(self.nc.psum_tensor(name, shape, dt))

    def phase(self):
        return PhaseScope(self.nc, self.shared)


class PhaseScope:

    def __init__(self, nc, shared):
        self.nc, self.shared = nc, shared

    def __enter__(self):
        self.ctx = ExitStack()
        self.ctx.__enter__()
        self.core = Core(self.nc, self.ctx, self.shared)
        return self.core

    def __exit__(self, kind, *rest):
        if kind is None:
            with self.nc.Block() as block:
                @block.gpsimd
                def _(pool):
                    for sem in self.core.sems:
                        pool.sem_clear(sem)
        return self.ctx.__exit__(kind, *rest)


def setup_phase(nc, top, g, dram):
    with top.phase() as c, nc.Block() as block:
        typ = c.sb("typ", [P, W], I32)
        tmp = c.sb("digits_tmp", [P, W], I32)
        s_w = c.sem("su_weights_loaded")
        s_a = c.sem("su_attention_loaded")
        s_st = c.sem("su_stats")
        s_norm = c.sem("su_norm_line")
        s_root = c.sem("su_root")
        weights = [(g.w0_node[:, :], dram.w0_node), (g.b0_msg[:, :], dram.b0_msg), (g.w0_edge[:, :], dram.w0_edge),
                   (g.w0_h[:, :], dram.w0_h), (g.w0_near[:, :], dram.w0_near), (g.b0_apply[:, :], dram.b0_apply),
                   (g.w1[:, :], dram.w1), (g.b1[:, :], dram.b1), (g.w2[:, :], dram.w2), (g.b2[:, :], dram.b2),
                   (g.wx[:, 0:D], dram.w_att_t), (g.w_att[:, :], dram.w_att), (g.w3[:, :], dram.w3)]
        s_zero = c.sem("su_zeroed")
        s_idx = c.sem("su_indices_loaded")
        s_x = [c.sem(f"su_x_loaded{n}") for n in range(XP)]
        s_const = c.sem("su_constants")
        s_v = c.sem("su_vector_line")
        line_sem = c.sem("su_pool_line")

        @block.gpsimd
        def _(pool):
            line = Line(pool, line_sem)
            for t in (g.src, g.dst, typ):
                pool.memset(t[:, STEPS:W], 0).then_inc(s_zero, 1)
            pool.memset(g.x[:, NT - 1, :], 0.0).then_inc(s_zero, 1)
            pool.memset(g.a_cols[:, :], 0.0).then_inc(s_zero, 1)
            line(pool.memset(g.ones[:, :], 1.0))
            line(pool.memset(g.ident[:, :], 0.0))
            line(pool.memset(g.identb[:, :], 0.0))
            for m in (g.ident, g.identb):
                line(pool.affine_select(out=m[:, :], in_=m[:, :], compare_op=ALU.not_equal, fill=1.0,
                                        base=0, pattern=[[-1, P]], channel_multiplier=1))
            line(pool.affine_select(out=g.before[:, :], in_=g.ones[:, :], compare_op=ALU.is_gt, fill=0.0,
                                    base=0, pattern=[[1, P]], channel_multiplier=-1))
            line(pool.affine_select(out=g.upto[:, :], in_=g.ones[:, :], compare_op=ALU.is_ge, fill=0.0,
                                    base=0, pattern=[[1, P]], channel_multiplier=-1))
            line(pool.affine_select(out=g.after[:, :], in_=g.ones[:, :], compare_op=ALU.is_gt, fill=0.0,
                                    base=0, pattern=[[-1, P]], channel_multiplier=1))
            line(pool.iota(g.row[:, :], [[1, P]], base=0, channel_multiplier=0,
                           allow_small_or_imprecise_dtypes=True))
            line(pool.iota(g.part[:, :], [[0, 1]], base=0, channel_multiplier=1,
                           allow_small_or_imprecise_dtypes=True))
            line(pool.iota(g.trash[:, :], [[0, 1]], base=E, channel_multiplier=1))
            pool.sem_inc(s_const, 1)

        @block.sync
        def _(sp):
            sp.wait_ge(s_zero, 5)
            for t, rows in ((g.src, dram.src), (g.dst, dram.dst), (typ, dram.edge_type_8)):
                long, short = chunked(rows.rearrange("(e o) -> e o", o=1))
                sp.dma_start(t[0:LONG, 0:STEPS + 1], long[:, :, 0]).then_inc(s_idx, 16)
                sp.dma_start(t[LONG:P, 0:STEPS], short[:, :, 0]).then_inc(s_idx, 16)
            for n in range(XP):
                a, b = n * NT // XP, (n + 1) * NT // XP
                if n == XP - 1:
                    b -= 1
                    sp.dma_start(g.x[0:TAIL, b, :], dram.x[b * P:N, :]).then_inc(s_x[n], 16)
                sp.dma_start(g.x[:, a:b, :], nodes(dram.x[a * P:b * P, :])).then_inc(s_x[n], 16)
            for to, rows in weights:
                sp.dma_start(to, rows).then_inc(s_w, 16)
            for h in range(HEADS):
                for n in range(2):
                    sp.dma_start(g.a_cols[h * HD:(h + 1) * HD, n * HEADS + h:n * HEADS + h + 1],
                                 dram.a_w[n * HD:(n + 1) * HD, :]).then_inc(s_a, 16)
            sp.wait_ge(s_w, 16 * len(weights))
            sp.wait_ge(s_a, 16 * 2 * HEADS)

        @block.scalar
        def _(act):
            act.wait_ge(s_norm, 6)
            nc.scalar.activation(g.shift[:, :], g.scale[:, :], ACT.Sqrt).then_inc(s_root, 1)

        @block.vector
        def _(dve):
            line = Line(dve, s_v)
            dve.wait_ge(s_idx, 6 * 16)
            line(dve.memset(g.keep[:, 0:1], 0.0))
            line(dve.tensor_tensor(g.keep[:, 1:W], g.dst[:, 1:W], g.dst[:, 0:W - 1], ALU.is_equal))
            for t, lo, hi in ((g.src, g.src_lo, g.src_hi), (g.dst, g.dst_lo, g.dst_hi)):
                line(dve.tensor_scalar(tmp[:, :], t[:, :], P - 1, None, ALU.bitwise_and))
                line(dve.tensor_copy(lo[:, :], tmp[:, :]))
                line(dve.tensor_scalar(tmp[:, :], t[:, :], 7, None, ALU.logical_shift_right))
                line(dve.tensor_copy(hi[:, :], tmp[:, :]))
            for word, (stride, ids) in enumerate(((NPAD, g.dst), (1 << RSHIFT, g.src))):
                line(dve.scalar_tensor_tensor(out=g.pay[:, :, word], in0=typ[:, :], scalar=float(stride), in1=ids[:, :],
                                              op0=ALU.mult, op1=ALU.add))
            dve.wait_ge(s_const, 1)
            line(dve.tensor_copy(g.rowb[:, :], g.row[:, :]))
            line(dve.tensor_scalar(g.chunk_start[:, :], g.part[:, :], float(LONG), None, ALU.min))
            line(dve.scalar_tensor_tensor(out=g.chunk_start[:, :], in0=g.part[:, :], scalar=float(STEPS),
                                          in1=g.chunk_start[:, :], op0=ALU.mult, op1=ALU.add))
            for n in range(XP):
                a, b = n * NT // XP, (n + 1) * NT // XP
                dve.wait_ge(s_x[n], 32 if n == XP - 1 else 16)
                for j in range(a, b):
                    ins = dve.bn_stats(g.stats[:, j, :], g.x[:, j, :])
                ins.then_inc(s_st, 1)
            dve.wait_ge(s_st, XP)
            norm_stats(Line(dve, s_norm), lambda: dve.wait_ge(s_root, 1), g)


class Boundaries:

    def __init__(self, c, g, tag, ids, seg, in_first):
        self.g, self.ids, self.seg, self.in_first = g, ids, seg, in_first
        self.count = c.sb(f"{tag}_count", [P, 1])
        self.diag = c.sb(f"{tag}_diag", [P, 2, P])
        self.spread = c.ps(f"{tag}_spread", [P, 2, P])
        self.s_diag = c.sem(f"{tag}_diagonals")
        self.s_row = c.sem(f"{tag}_rows_spread")

    def vector(self, line):
        dve, g, ids, seg = line.eng, self.g, self.ids, self.seg
        line(dve.tensor_copy(seg.first[:, :], ids[:, 0:1]))
        line(dve.tensor_copy(seg.last[0:LONG, :], ids[0:LONG, STEPS:STEPS + 1]))
        line(dve.tensor_copy(seg.last[LONG:P, :], ids[LONG:P, STEPS - 1:STEPS]))
        for n, end in enumerate((seg.first, seg.last)):
            dve.tensor_scalar(self.diag[:, n, :], g.ident[:, :], end[:, 0:1], None, ALU.mult).then_inc(self.s_diag, 1)
        line(dve.tensor_scalar(self.in_first[:, :], ids[:, 0:STEPS + 1], seg.first[:, 0:1], None, ALU.is_equal))
        line(dve.memset(self.in_first[LONG:P, STEPS:STEPS + 1], 0.0))
        line(dve.tensor_reduce(self.count[:, :], self.in_first[:, :], AX.X, ALU.add))
        line(dve.scalar_tensor_tensor(out=seg.first_end[:, :], in0=self.count[:, :], scalar=-1.0,
                                      in1=g.chunk_start[:, :], op0=ALU.add, op1=ALU.add))
        dve.wait_ge(self.s_row, 1)
        line(dve.scalar_tensor_tensor(out=seg.carry_mask[:, :], in0=self.spread[:, 0, :], scalar=seg.last[:, 0:1],
                                      in1=g.before[:, :], op0=ALU.is_equal, op1=ALU.mult))
        line(dve.scalar_tensor_tensor(out=seg.carry_mask_t[:, :], in0=self.spread[:, 1, :], scalar=seg.first[:, 0:1],
                                      in1=g.after[:, :], op0=ALU.is_equal, op1=ALU.mult))

    def tensor(self, pe):
        pe.wait_ge(self.s_diag, 2)
        pe.matmul(self.spread[:, 0, :], self.g.ones[:, :], self.diag[:, 0, :], start=True, stop=True)
        pe.matmul(self.spread[:, 1, :], self.g.ones[:, :], self.diag[:, 1, :], start=True, stop=True).then_inc(self.s_row, 1)


def boundary_phase(nc, top, g, dram):
    with top.phase() as c, nc.Block() as block:
        bounds = Boundaries(c, g, "bd", g.dst, g.dst_seg, c.sb("bd_in_first", [P, STEPS + 1]))
        zero = c.sb("bd_zero_rows", [P, W])
        ps = c.ps("bd_scores", [P, 2 * HEADS])
        bias = c.ps("bd_bias", [P, 3, D])
        s_zero = c.sem("bd_zeroed")
        s_z = c.sem("bd_zero_rows_written")
        s_v = c.sem("bd_vector_line")
        s_m = c.sem("bd_products_ready")
        s_c = c.sem("bd_products_copied")

        @block.gpsimd
        def _(pool):
            pool.memset(zero[:, :], 0.0).then_inc(s_zero, 1)

        @block.sync
        def _(sp):
            zero_rows = dram.dst_terms[0:E].rearrange("e h -> (e h)").rearrange("(p w) -> p w", p=P)
            width, piece = zero_rows.shape[1], zero.shape[1]
            sp.wait_ge(s_zero, 1)
            for at in range(0, width, piece):
                n = min(piece, width - at)
                sp.dma_start(zero_rows[:, at:at + n], zero[:, 0:n]).then_inc(s_z, 16)
            sp.wait_ge(s_z, 16 * -(-width // piece))

        @block.vector
        def _(dve):
            bounds.vector(Line(dve, s_v))

        @block.scalar
        def _(act):
            act.wait_ge(s_m, 2)
            nc.scalar.copy(g.wx[:, D:D + 2 * HEADS], ps[:, :]).then_inc(s_c, 1)
            nc.scalar.copy(g.bias_rows[:, :, :], bias[:, :, :]).then_inc(s_c, 1)

        @block.tensor
        def _(pe):
            pe.matmul(ps[:, :], g.w_att[:, :], g.a_cols[:, :], start=True, stop=True).then_inc(s_m, 1)
            for n, b in enumerate((g.b0_msg, g.b0_apply, g.b2)):
                ins = pe.matmul(bias[:, n, :], g.ones[0:1, :], b[0:1, :], start=True, stop=True)
            ins.then_inc(s_m, 1)
            bounds.tensor(pe)


def norm_stats(line, wait_root, g):
    dve = line.eng
    st = g.stats
    line(dve.tensor_tensor(g.mean[:, :], st[:, :, 1], st[:, :, 4], ALU.add))
    line(dve.tensor_tensor(g.scale[:, :], st[:, :, 1], st[:, :, 4], ALU.subtract))
    line(dve.scalar_tensor_tensor(out=g.scale[:, :], in0=g.scale[:, :], scalar=0.25, in1=g.scale[:, :],
                                  op0=ALU.mult, op1=ALU.mult))
    line(dve.tensor_tensor(g.shift[:, :], st[:, :, 2], st[:, :, 5], ALU.add))
    line(dve.scalar_tensor_tensor(out=g.scale[:, :], in0=g.shift[:, :], scalar=1.0 / D, in1=g.scale[:, :],
                                  op0=ALU.mult, op1=ALU.add))
    line(dve.tensor_scalar(g.scale[:, :], g.scale[:, :], EPS, None, ALU.add))
    wait_root()
    line(dve.reciprocal(g.scale[:, :], g.shift[:, :]))
    line(dve.scalar_tensor_tensor(out=g.shift[:, :], in0=g.mean[:, :], scalar=-0.5, in1=g.scale[:, :],
                                  op0=ALU.mult, op1=ALU.mult))


def normalise(nc, g, out, j, k, done):
    one = bass.ds(j + k, 1)
    nc.scalar.activation(out[:, k:k + 1, :], g.x[:, one, :], ACT.Relu, bias=g.shift[:, one],
                         scale=g.scale[:, one]).then_inc(done, 1)


def project_phase_0(nc, top, g, dram):
    with top.phase() as c, nc.Block() as block:
        h = c.sb("p0_h", [P, 2, KN, D])
        ht = c.sb("p0_h_transposed", [P, 2, KN * D])
        out = c.sb("p0_out", [P, 2, KN, D])
        tp = c.ps("p0_transposes", [P, 2, 1024])
        mm = c.ps("p0_products", [P, 2, 1024])
        s_h = c.sem("p0_h_ready")
        s_t = c.sem("p0_transposed")
        s_tc = c.sem("p0_transposes_copied")
        s_m = c.sem("p0_products_ready")
        s_o = c.sem("p0_out_ready")
        s_w = [c.sem(f"p0_written{s}") for s in range(2)]
        later = lambda i: not isinstance(i, int) or i > 0
        at = lambda i, s: 2 * i + s

        @block.scalar
        def _(act):
            def norm(i, s):
                if later(i):
                    act.wait_ge(s_t, at(i, s) - 1)
                for k in range(KN):
                    normalise(nc, g, h[:, s], KN * at(i, s), k, s_h)
            batches(act, NNB, norm)

        @block.vector
        def _(dve):
            def copy_transposes(i, s):
                dve.wait_ge(s_t, at(i, s) + 1)
                if later(i):
                    dve.wait_ge(s_m, at(i, s) - 1)
                dve.tensor_copy(ht[:, s, :], tp[:, s, 0:KN * D]).then_inc(s_tc, 1)

            def copy_out(i, s):
                dve.wait_ge(s_m, at(i, s) + 1)
                if later(i):
                    dve.wait_ge(s_w[s], 16 * i)
                dve.tensor_tensor(out[:, s, :, :], mm[:, s, 0:KN * D].rearrange("p (k d) -> p k d", k=KN),
                                  g.bias_rows[:, 0, :].unsqueeze(1).to_broadcast([P, KN, D]), ALU.add).then_inc(s_o, 1)
            lagged(dve, NNB, [(copy_transposes, 0), (copy_out, 1)])

        @block.tensor
        def _(pe):
            def transposes(i, s):
                if later(i):
                    pe.wait_ge(s_tc, at(i, s) - 1)
                for k in range(KN):
                    pe.wait_ge(s_h, KN * at(i, s) + k + 1)
                    ins = pe.transpose(tp[:, s, k * D:(k + 1) * D], h[:, s, k, :], g.ident[:, :])
                ins.then_inc(s_t, 1)

            def products(i, s):
                pe.wait_ge(s_tc, at(i, s) + 1)
                if later(i):
                    pe.wait_ge(s_o, at(i, s) - 1)
                for k in range(KN):
                    ins = pe.matmul(mm[:, s, k * D:(k + 1) * D], ht[:, s, k * D:(k + 1) * D], g.w0_node[:, :],
                                    start=True, stop=True)
                ins.then_inc(s_m, 1)
            lagged(pe, NNB, [(transposes, 0), (products, 1)])

        @block.sync
        def _(sp):
            def write(i, s):
                sp.wait_ge(s_o, at(i, s) + 1)
                sp.dma_start(nodes(dram.table0)[:, bass.ds(KN * at(i, s), KN), :], out[:, s, :, :]).then_inc(s_w[s], 16)
            batches(sp, NNB, write)
            for s in range(2):
                sp.wait_ge(s_w[s], 16 * (NNB // 2))


def norm_phase_1(nc, top, g, dram):
    with top.phase() as c, nc.Block() as block:
        h = c.sb("p1_h", [P, NT, D])
        mine = 4
        s_h = c.sem("p1_h_by_scalar")
        s_n = c.sem("p1_normed_by_vector")
        s_hv = c.sem("p1_h_by_vector")
        s_w = c.sem("p1_written")

        @block.scalar
        def _(act):
            with act.Fori(0, NNB) as b:
                for k in range(mine):
                    one = bass.ds(KN * b + k, 1)
                    nc.scalar.activation(h[:, one, :], g.x[:, one, :], ACT.Relu, bias=g.shift[:, one],
                                         scale=g.scale[:, one]).then_inc(s_h, 1)

        @block.vector
        def _(dve):
            def body(i, s):
                for k in range(mine, KN):
                    one = bass.ds(KN * (2 * i + s) + k, 1)
                    ins = dve.tensor_scalar(h[:, one, :], g.x[:, one, :], g.scale[:, one], g.shift[:, one],
                                            ALU.mult, ALU.add)
                ins.then_inc(s_n, 1)
                dve.wait_ge(s_n, 2 * i + s + 1)
                rest = h[:, bass.ds(KN * (2 * i + s) + mine, KN - mine), :].rearrange("p k d -> p (k d)")
                dve.tensor_scalar(rest, rest, 0.0, None, ALU.max).then_inc(s_hv, 1)
            batches(dve, NNB, body)

        @block.sync
        def _(sp):
            def body(i, s):
                sp.wait_ge(s_h, mine * (2 * i + s + 1))
                sp.wait_ge(s_hv, 2 * i + s + 1)
                sp.dma_start(nodes(dram.table0)[:, bass.ds(KN * (2 * i + s), KN), :],
                             h[:, bass.ds(KN * (2 * i + s), KN), :]).then_inc(s_w, 16)
            batches(sp, NNB, body)
            sp.wait_ge(s_w, 16 * NNB)


def project_phase(nc, top, g, tag, table, weights, cols, out_cols, copy_act, copy_dve=None,
                  prepare=None, terms=None, beside=None):
    with top.phase() as c, nc.Block() as block:
        beside = beside and beside(c)
        h = c.sb(f"{tag}_h", [P, 2, KN, D])
        s_h = c.sem(f"{tag}_h_ready")
        s_w = [c.sem(f"{tag}_written{s}") for s in range(KN if beside else 2)]
        ht = c.sb(f"{tag}_h_transposed", [P, 2, KN, D])
        out = c.sb(f"{tag}_out", [P, 1 if beside else 2, KN, out_cols])
        tp = c.ps(f"{tag}_transposes", [P, 2 * 512])
        split = D if cols < 512 else 512
        parts = [(at, min(split, cols - at), 512 * n) for n, at in enumerate(range(0, cols, split))]
        mm = c.ps(f"{tag}_products", [P, 2, 512 * len(parts)])
        s_pre = c.sem(f"{tag}_prepared")
        s_t = c.sem(f"{tag}_transposed")
        s_tc = c.sem(f"{tag}_transposes_copied")
        s_m = c.sem(f"{tag}_products_ready")
        s_e = c.sem(f"{tag}_products_copied_by_scalar")
        s_e2 = c.sem(f"{tag}_products_copied_by_vector")
        if terms:
            term = c.sb(f"{tag}_terms", [P, 2, KN, HEADS])
            term_row = c.sb(f"{tag}_term_rows", [P, 2, KN], I32)
            s_row = c.sem(f"{tag}_term_rows_staged")
            s_go = c.sem(f"{tag}_scatter_go")
            s_scat = [c.soft(f"{tag}_terms_scattered{s}") for s in range(2)]
            s_nt = [c.sem(f"{tag}_node_terms_written{s}") for s in range(2)]

            @block.gpsimd
            def _(pool):
                def body(i, s):
                    pool.wait_ge(s_row, 2 * i + s + 1)
                    pool.wait_ge(s_e2, 2 * KN * i + (s + 1) * KN)
                    pool.sem_inc(s_go, 1)
                    for k in range(KN):
                        pool.indirect_dma_start(
                            out=terms.dst_terms[:, :], in_=term[:, s, k, :], in_offset=None,
                            out_offset=bass.IndirectOffsetOnAxis(ap=term_row[:, s, k:k + 1], axis=0)
                        ).then_inc(s_scat[s], 16)
                batches(pool, NNB, body)
                for s in range(2):
                    pool.wait_ge(s_scat[s], 16 * KN * (NNB // 2))

        later = lambda i: not isinstance(i, int) or i > 0

        @block.scalar
        def _(act):
            def norm(i, s):
                if later(i):
                    act.wait_ge(s_t, 2 * i + s - 1)
                for k in range(KN):
                    normalise(nc, g, h[:, s], KN * (2 * i + s), k, s_h)

            def copy_transposes(i, s):
                act.wait_ge(s_t, 2 * i + s + 1)
                if later(i):
                    act.wait_ge(s_m, (2 * i + s - 1) * KN)
                for a, b in GN:
                    ins = nc.scalar.copy(ht[:, s, a:b, :].rearrange("p k d -> p (k d)"), tp[:, a * D:b * D])
                ins.then_inc(s_tc, 1)

            def copy_out(i, s):
                if later(i) and not beside:
                    act.wait_ge(s_w[s], i * 16)
                for k in range(KN):
                    if beside and (later(i) or s):
                        act.wait_ge(s_w[k], 16 * (2 * i + s))
                    act.wait_ge(s_m, 2 * KN * i + s * KN + k + 1)
                    copy_act(out[:, 0 if beside else s, k, :], mm[:, (s * KN + k) % 2, :]).then_inc(s_e, 1)
            if beside:
                lagged(act, NNB, [(copy_transposes, 1), (norm, 0), (copy_out, 2)])
            else:
                act.wait_ge(s_pre, 1)
                lagged(act, NNB, [(norm, 0), (copy_out, 2)])

        @block.vector
        def _(dve):
            if beside:
                beside.vector(dve)
                return
            if prepare is not None:
                prepare(dve, out, s_pre)
            else:
                dve.sem_inc(s_pre, 1)

            def copy_transposes(i, s):
                dve.wait_ge(s_t, 2 * i + s + 1)
                if later(i):
                    dve.wait_ge(s_m, (2 * i + s - 1) * KN)
                dve.tensor_copy(ht[:, s, :, :].rearrange("p k d -> p (k d)"), tp[:, 0:KN * D]).then_inc(s_tc, 1)

            def copy_out(i, s):
                if copy_dve is not None:
                    if later(i):
                        dve.wait_ge(s_w[s], i * 16)
                        if terms:
                            dve.wait_ge(s_scat[s], i * 16 * KN)
                            dve.wait_ge(s_nt[s], i * 16)
                    if terms:
                        dve.tensor_copy(term_row[:, s, :], g.term_row[:, bass.ds(2 * KN * i + s * KN, KN)]).then_inc(s_row, 1)
                    for k in range(KN):
                        dve.wait_ge(s_m, 2 * KN * i + s * KN + k + 1)
                        product = mm[:, (s * KN + k) % 2, :]
                        if terms:
                            dve.tensor_copy(term[:, s, k, :], product[:, 512 + HEADS:512 + 2 * HEADS])
                        copy_dve(out[:, s, k, :], product).then_inc(s_e2, 1)
            lagged(dve, NNB, [(copy_transposes, 0), (copy_out, 1)])

        @block.tensor
        def _(pe):
            def transposes(i, s):
                if later(i) or s:
                    pe.wait_ge(s_tc, 2 * i + s)
                for k in range(KN):
                    pe.wait_ge(s_h, 2 * KN * i + s * KN + k + 1)
                    ins = pe.transpose(tp[:, k * D:(k + 1) * D], h[:, s, k, :], g.ident[:, :])
                ins.then_inc(s_t, 1)

            def products(i, s):
                pe.wait_ge(s_tc, 2 * i + s + 1)
                for k in range(KN):
                    j = 2 * KN * i + s * KN + k
                    if not isinstance(i, int) or j >= 2:
                        pe.wait_ge(s_e, j - 1)
                        if copy_dve is not None:
                            pe.wait_ge(s_e2, j - 1)
                    for at, n, bank in parts:
                        to = mm[:, (s * KN + k) % 2, bank:bank + n]
                        ins = pe.matmul(to, ht[:, s, k, :], weights[:, at:at + n], start=True, stop=True)
                    ins.then_inc(s_m, 1)
                if beside and isinstance(i, int):
                    beside.tensor(pe, 2 * i + s)
            lagged(pe, NNB, [(transposes, 0), (products, 1)])

        @block.sync
        def _(sp):
            def body(i, s):
                if beside:
                    for k in range(KN):
                        j = 2 * KN * i + s * KN + k
                        sp.wait_ge(s_e, j + 1)
                        sp.dma_start(table(j, 1), out[:, 0, k, :].rearrange("p (r d) -> p r d", r=REL)).then_inc(s_w[k], 16)
                    return
                sp.wait_ge(s_e, 2 * KN * i + (s + 1) * KN)
                if copy_dve is not None:
                    sp.wait_ge(s_e2, 2 * KN * i + (s + 1) * KN)
                if terms:
                    sp.dma_start(nodes(terms.node_terms)[:, bass.ds(2 * KN * i + s * KN, KN), :],
                                 term[:, s, :, :]).then_inc(s_nt[s], 16)
                sp.dma_start(table(2 * KN * i + s * KN, KN), out[:, s, :, :]).then_inc(s_w[s], 16)
            if beside:
                beside.sync(sp)
            batches(sp, NNB, body)
            for sem in s_w:
                sp.wait_ge(sem, 16 * (NNB if beside else NNB // 2))
            if terms:
                for s in range(2):
                    sp.wait_ge(s_nt[s], 16 * (NNB // 2))


class EdgePhase:

    def __init__(self, nc, top, c, g, tag, table, rows_dram, width):
        self.nc, self.g, self.tag, self.table, self.width = nc, g, tag, table, width
        self.rows_dram = rows_dram
        self.index = c.sb(f"{tag}_index", [P, 2, K], I32)
        self.gathered = c.sb(f"{tag}_gathered", [P, 2, K, width])
        self.rows = c.sb(f"{tag}_rows", [P, 2, K, width])
        self.s_index = c.sem(f"{tag}_index_staged")
        self.s_gat = [c.soft(f"{tag}_gathered{s}") for s in range(2)]
        self.s_used = c.sem(f"{tag}_gathered_used") if tag != "e0" else None
        self.s_go = c.sem(f"{tag}_gather_slot_free")
        self.s_rows = c.sem(f"{tag}_rows_summed")
        self.s_out = [c.sem(f"{tag}_rows_written{s}") for s in range(2)]

    def run(self, eng, body):
        batches(eng, NB, lambda i, s: body(i, s, K))
        body(NB // 2, 0, 1)

    def gather(self, pool):
        def body(i, s, n):
            pool.wait_ge(self.s_index, 2 * i + s + 1)
            if not isinstance(i, int) or i > 0:
                pool.wait_ge(self.s_used, 2 * i + s - 1)
            pool.sem_inc(self.s_go, 1)
            for k in range(n):
                pool.indirect_dma_start(
                    out=self.gathered[:, s, k, :], out_offset=None, in_=self.table,
                    in_offset=bass.IndirectOffsetOnAxis(ap=self.index[:, s, k:k + 1], axis=0)).then_inc(self.s_gat[s], 16)
        self.run(pool, body)

    def wait_gathered(self, eng, i, s, n):
        eng.wait_ge(self.s_gat[s], 16 * K * i + 16 * n)

    def stage_first(self, act, ids):
        for s in range(2):
            self.nc.scalar.copy(self.index[:, s, :], ids[:, s * K:(s + 1) * K]).then_inc(self.s_index, 1)

    def stage_next(self, act, ids, i, s, n):
        if n == K:
            self.nc.scalar.copy(self.index[:, s, :], ids[:, bass.ds(2 * K * i + (s + 2) * K, K)]).then_inc(self.s_index, 1)

    def wait_rows_out(self, eng, i, s):
        if not isinstance(i, int) or i > 0:
            eng.wait_ge(self.s_out[s], 32 * i)

    def write_rows(self, sp, i, s, n):
        sp.wait_ge(self.s_rows, 2 * K * i + s * K + n)
        long, short = chunked(self.rows_dram)
        sp.dma_start(long[:, bass.ds(2 * K * i + s * K, K), :], self.rows[0:LONG, s, :, :]).then_inc(self.s_out[s], 16)
        sp.dma_start(short[:, bass.ds(2 * K * i + s * K, K), :], self.rows[LONG:P, s, :, :]).then_inc(self.s_out[s], 16)

    def write_last(self, sp):
        sp.wait_ge(self.s_rows, STEPS + 1)
        long, _ = chunked(self.rows_dram)
        sp.dma_start(long[:, STEPS, :], self.rows[0:LONG, 0, 0, :]).then_inc(self.s_out[0], 16)
        sp.wait_ge(self.s_out[0], 32 * (NB // 2) + 16)
        sp.wait_ge(self.s_out[1], 32 * (NB // 2))

    def write_behind(self, sp, i, s, n, load):
        load(i, s, n)
        if isinstance(i, int) and i == 0 and s == 0:
            return
        if s:
            self.write_rows(sp, i, 0, K)
        else:
            self.write_rows(sp, i - 1, 1, K)

    def previous(self, s, k):
        return self.rows[:, s, k - 1] if k else self.rows[:, 1 - s, K - 1]

    def sum_steps(self, dve, keep_stage, i, s, n):
        for k in range(n):
            dve.scalar_tensor_tensor(out=self.rows[:, s, k], in0=self.previous(s, k), scalar=keep_stage[:, s, k:k + 1],
                                     in1=self.rows[:, s, k], op0=ALU.mult, op1=ALU.add).then_inc(self.s_rows, 1)
            dve.wait_ge(self.s_rows, 2 * K * i + s * K + k + 1)

    def keep_ends(self, dve, tail, s_tail):
        dve.tensor_copy(tail[0:LONG], self.rows[0:LONG, 0, 0]).then_inc(s_tail, 1)
        dve.tensor_copy(tail[LONG:P], self.rows[LONG:P, 1, K - 1]).then_inc(s_tail, 1)


def edge_phase_0(nc, top, g, dram):
    with top.phase() as c, nc.Block() as block:
        e = EdgePhase(nc, top, c, g, "e0", dram.table0[:, :], dram.rows[:, :], D)
        feat = c.sb("e0_features", [DE, 2, K, P])
        keep = c.sb("e0_keep", [P, 2, K])
        hot = [[c.sb(f"e0_{nm}_{dg}_hot", [P, 2, K, n], BF16) for dg, n in (("low", P), ("high", NT))]
               for nm in ("src", "dst")]
        z = c.ps("e0_messages", [P, 2, 3 * 512])
        hist = [c.ps("e0_src_histogram", [P, 512]), c.ps("e0_dst_histogram", [P, 512])]
        s_feat = [c.sem(f"e0_features_loaded{s}") for s in range(2)]
        s_msg = c.sem("e0_messages_ready")
        s_keep = c.sem("e0_keep_staged")
        s_hot = c.sem("e0_digits_hot")
        s_hist = c.sem("e0_histograms_counted")
        s_relu = c.sem("e0_relu_done")
        s_tail = c.sem("e0_tail")
        s_zero = c.sem("e0_zeroed")
        e.s_used = s_msg

        @block.gpsimd
        def _(pool):
            e.gather(pool)

        @block.sync
        def _(sp):
            def load(i, s, n):
                if not isinstance(i, int) or i > 0:
                    sp.wait_ge(s_msg, 2 * i + s - 1)
                sp.dma_start(feat[:, s, 0:n, :], dram.edge64_t[:, bass.ds(2 * K * i + s * K, n), :]).then_inc(s_feat[s], 16)
            e.run(sp, lambda i, s, n: e.write_behind(sp, i, s, n, load))
            e.write_last(sp)

        @block.scalar
        def _(act):
            e.stage_first(act, g.src)

            def body(i, s, n):
                e.wait_gathered(act, i, s, n)
                e.stage_next(act, g.src, i, s, n)
                act.wait_ge(s_msg, 2 * i + s + 1)
                e.wait_rows_out(act, i, s)
                if not isinstance(i, int) or i or s:
                    act.wait_ge(e.s_rows, 2 * K * i + (s - 1) * K + 1)
                for a, b in GK:
                    b = min(b, n)
                    if a < b:
                        ins = nc.scalar.activation(e.rows[:, s, a:b, :].rearrange("p k d -> p (k d)"),
                                                   z[:, s, a * D:b * D], ACT.Relu)
                ins.then_inc(s_relu, 1)
            act.wait_ge(s_zero, 1)
            e.run(act, body)

        @block.vector
        def _(dve):
            dve.memset(e.rows[:, 1, K - 1, :], 0.0).then_inc(s_zero, 1)
            dve.wait_ge(s_zero, 1)

            def body(i, s, n):
                b = 2 * K * i + s * K
                dve.tensor_copy(keep[:, s, 0:n], g.keep[:, bass.ds(b, n)]).then_inc(s_keep, 1)
                if not isinstance(i, int) or i > 0:
                    dve.wait_ge(s_hist, 2 * i + s - 1)
                for (lo, hi), (lo_hot, hi_hot) in zip(((g.src_lo, g.src_hi), (g.dst_lo, g.dst_hi)), hot):
                    for digit, to, m in ((lo, lo_hot, P), (hi, hi_hot, NT)):
                        dve.tensor_tensor(to[:, s, 0:n, :], digit[:, bass.ds(b, n)].unsqueeze(2).to_broadcast([P, n, m]),
                                          g.rowb[:, 0:m].unsqueeze(1).to_broadcast([P, n, m]), ALU.is_equal).then_inc(s_hot, 1)
                dve.wait_ge(s_keep, 2 * i + s + 1)
                dve.wait_ge(s_relu, 2 * i + s + 1)
                e.sum_steps(dve, keep, i, s, n)
            e.run(dve, body)
            e.keep_ends(dve, g.tail[:, 0:D], s_tail)
            dve.wait_ge(s_hist, NB + 1)
            dve.tensor_copy(g.src_hist[:, :], hist[0][:, 0:NT])
            dve.tensor_copy(g.dst_hist[:, :], hist[1][:, 0:NT])

        @block.tensor
        def _(pe):
            def body(i, s, n):
                e.wait_gathered(pe, i, s, n)
                pe.wait_ge(s_feat[s], 16 * (i + 1))
                if not isinstance(i, int) or i > 0:
                    pe.wait_ge(s_relu, 2 * i + s - 1)
                for a, b in GK:
                    b = min(b, n)
                    if a < b:
                        pe.matmul(z[:, s, a * D:b * D], g.ident[:, :],
                                  e.gathered[:, s, a:b, :].rearrange("p k d -> p (k d)"), start=True, stop=False,
                                  skip_group_check=True)
                        for k in range(a, b):
                            ins = pe.matmul(z[:, s, k * D:(k + 1) * D], feat[:, s, k, :], g.w0_edge[:, :],
                                            start=False, stop=True, skip_group_check=True)
                ins.then_inc(s_msg, 1)
                pe.wait_ge(s_hot, 8 * i + 4 * s + 4)
                q = P if n == K else LONG
                for to, (lo_hot, hi_hot) in zip(hist, hot):
                    for k in range(n):
                        first = isinstance(i, int) and i == 0 and s == 0 and k == 0
                        ins = pe.matmul(to[:, 0:NT], lo_hot[0:q, s, k, :], hi_hot[0:q, s, k, :],
                                        start=first, stop=n == 1, skip_group_check=True)
                ins.then_inc(s_hist, 1)
            e.run(pe, body)


def edge_phase_1(nc, top, g, dram):
    with top.phase() as c, nc.Block() as block:
        e = EdgePhase(nc, top, c, g, "e1", dram.table0[:, :], dram.rows[:, :], D)
        feat = c.sb("e1_features", [P, 2, K, D])
        keep = c.sb("e1_keep", [P, 2, K])
        s_feat = [c.sem(f"e1_features_loaded{s}") for s in range(2)]
        s_keep = c.sem("e1_keep_staged")
        s_tail = c.sem("e1_tail")
        s_zero = c.sem("e1_zeroed")

        @block.gpsimd
        def _(pool):
            e.gather(pool)

        @block.sync
        def _(sp):
            long, short = chunked(dram.edge_attr_128)

            def load(i, s, n):
                if not isinstance(i, int) or i > 0:
                    sp.wait_ge(e.s_used, 2 * i + s - 1)
                sp.dma_start(feat[0:LONG, s, 0:n, :], long[:, bass.ds(2 * K * i + s * K, n), :]).then_inc(s_feat[s], 16)
                if n == K:
                    sp.dma_start(feat[LONG:P, s, :, :], short[:, bass.ds(2 * K * i + s * K, n), :]).then_inc(s_feat[s], 16)
            e.run(sp, lambda i, s, n: e.write_behind(sp, i, s, n, load))
            e.write_last(sp)

        @block.scalar
        def _(act):
            e.stage_first(act, g.src)

            def body(i, s, n):
                e.wait_gathered(act, i, s, n)
                e.stage_next(act, g.src, i, s, n)
            e.run(act, body)

        @block.vector
        def _(dve):
            dve.memset(e.rows[:, 1, K - 1, :], 0.0).then_inc(s_zero, 1)
            dve.wait_ge(s_zero, 1)

            def body(i, s, n):
                dve.tensor_copy(keep[:, s, 0:n], g.keep[:, bass.ds(2 * K * i + s * K, n)]).then_inc(s_keep, 1)
                e.wait_gathered(dve, i, s, n)
                dve.wait_ge(s_feat[s], 32 * i + (32 if n == K else 16))
                e.wait_rows_out(dve, i, s)
                dve.tensor_tensor(e.rows[:, s, 0:n, :], e.gathered[:, s, 0:n, :], feat[:, s, 0:n, :],
                                  ALU.add).then_inc(e.s_used, 1)
                dve.wait_ge(s_keep, 2 * i + s + 1)
                dve.wait_ge(e.s_used, 2 * i + s + 1)
                e.sum_steps(dve, keep, i, s, n)
            e.run(dve, body)
            e.keep_ends(dve, g.tail[:, 0:D], s_tail)


def edge_phase_2(nc, top, g, dram):
    with top.phase() as c, nc.Block() as block:
        e = EdgePhase(nc, top, c, g, "e2", dram.table2[:, :], dram.rows2[:, :], AW)
        keep = c.sb("e2_keep", [P, 2, K])
        far = c.sb("e2_far", [P, K + 1])
        score = c.sb("e2_scores", [P, K, HEADS])
        running = c.sb("e2_running_max", [P, K, HEADS])
        m = c.sb("e2_max", [P, K, HEADS])
        m_before = c.sb("e2_max_before", [P, HEADS])
        power = c.sb("e2_exponents", [P, K + 1, HEADS])
        factor = c.sb("e2_factors", [P, K + 1, HEADS])
        kept = c.sb("e2_kept", [P, HEADS, HD + 1])
        s_v = c.sem("e2_vector_line")
        s_pow = c.sem("e2_exponents_ready")
        s_exp = c.sem("e2_factors_ready")
        s_kept = c.sem("e2_previous_scaled")
        s_tail = c.sem("e2_tail")
        s_zero = c.sem("e2_zeroed")
        per_head = lambda ap: ap.rearrange("p k (h w) -> p k h w", h=HEADS)
        LINKS = 4 + 2 * HEADS + 3

        @block.gpsimd
        def _(pool):
            e.gather(pool)

        @block.sync
        def _(sp):
            e.run(sp, lambda i, s, n: e.write_behind(sp, i, s, n, lambda *a: None))
            e.write_last(sp)

        @block.scalar
        def _(act):
            e.stage_first(act, g.src)

            def body(i, s, n):
                e.wait_gathered(act, i, s, n)
                e.stage_next(act, g.src, i, s, n)
                act.wait_ge(s_pow, 2 * i + s + 1)
                if not isinstance(i, int) or i or s:
                    act.wait_ge(s_kept, 2 * i + s)
                nc.scalar.activation(factor[:, 0:n + 1, :], power[:, 0:n + 1, :], ACT.Exp).then_inc(s_exp, 1)
            e.run(act, body)

        @block.vector
        def _(dve):
            dve.memset(far[:, :], 0.0).then_inc(s_zero, 1)
            dve.memset(m_before[:, :], 0.0).then_inc(s_zero, 1)
            dve.memset(e.rows[:, 1, K - 1, :], 0.0).then_inc(s_zero, 1)
            dve.wait_ge(s_zero, 3)
            line = Line(dve, s_v)

            def body(i, s, n):
                line.at(2 * LINKS * i + s * LINKS)
                b = 2 * K * i + s * K
                G = per_head(e.gathered[:, s, 0:n, :])
                R = per_head(e.rows[:, s, 0:n, :])
                line(dve.tensor_copy(keep[:, s, 0:n], g.keep[:, bass.ds(b, n)]))
                line(dve.tensor_scalar(far[:, 0:n], keep[:, s, 0:n], -1.0, FAR, ALU.add, ALU.mult))
                e.wait_gathered(dve, i, s, n)
                line(dve.tensor_tensor(score[:, 0:n, :], G[:, :, :, HD + 1], g.sdst[:, bass.ds(b, n), :], ALU.add))
                line(dve.scalar_tensor_tensor(out=score[:, 0:n, :], in0=score[:, 0:n, :], scalar=SLOPE,
                                              in1=score[:, 0:n, :], op0=ALU.mult, op1=ALU.max))
                for h in range(HEADS):
                    line(dve.tensor_tensor_scan(running[:, 0:n, h], far[:, 0:n], score[:, 0:n, h],
                                                m_before[:, h:h + 1], ALU.add, ALU.max))
                for h in range(HEADS):
                    line(dve.tensor_tensor_scan(m[:, 0:n, h][:, ::-1], far[:, 1:n + 1][:, ::-1],
                                                running[:, 0:n, h][:, ::-1], -FAR, ALU.add, ALU.max))
                line(dve.scalar_tensor_tensor(out=power[:, 0, :], in0=m_before[:, :], scalar=far[:, 0:1],
                                              in1=m[:, 0, :], op0=ALU.add, op1=ALU.subtract))
                line(dve.tensor_copy(m_before[:, :], m[:, n - 1, :]))
                dve.tensor_tensor(power[:, 1:n + 1, :], score[:, 0:n, :], m[:, 0:n, :], ALU.subtract).then_inc(s_pow, 1)
                e.wait_rows_out(dve, i, s)
                line(dve.tensor_copy(R[:, :, :, HD + 1], m[:, 0:n, :]))
                dve.wait_ge(s_exp, 2 * i + s + 1)
                dve.tensor_tensor(R[:, :, :, 0:HD + 1].rearrange("p k h w -> p (k h) w"),
                                  G[:, :, :, 0:HD + 1].rearrange("p k h w -> p (k h) w"),
                                  factor[:, 1:n + 1, :].rearrange("p k h -> p (k h)").unsqueeze(2)
                                  .to_broadcast([P, n * HEADS, HD + 1]), ALU.mult).then_inc(e.s_used, 1)
                sums = lambda row: row.rearrange("p (h w) -> p h w", h=HEADS)[:, :, 0:HD + 1]
                dve.tensor_tensor(kept[:, :, :], sums(e.previous(s, 0)),
                                  factor[:, 0, :].unsqueeze(2).to_broadcast([P, HEADS, HD + 1]),
                                  ALU.mult).then_inc(s_kept, 1)
                dve.wait_ge(s_kept, 2 * i + s + 1)
                dve.wait_ge(e.s_used, 2 * i + s + 1)
                for k in range(n):
                    row = sums(e.rows[:, s, k])
                    if k == 0:
                        ins = dve.tensor_tensor(row, row, kept[:, :, :], ALU.add)
                    else:
                        ins = dve.scalar_tensor_tensor(out=row, in0=sums(e.previous(s, k)), scalar=keep[:, s, k:k + 1],
                                                       in1=row, op0=ALU.mult, op1=ALU.add)
                    ins.then_inc(e.s_rows, 1)
                    dve.wait_ge(e.s_rows, 2 * K * i + s * K + k + 1)
                assert line.n == LINKS, line.n
            e.run(dve, body)
            e.keep_ends(dve, g.tail, s_tail)


def edge_phase_3(nc, top, g, dram):
    with top.phase() as c, nc.Block() as block:
        e = EdgePhase(nc, top, c, g, "e3", dram.table3[:, :], dram.rows[:, :], D)
        keep = c.sb("e3_keep", [P, 2, K])
        weight = c.sb("e3_weight", [P, 2, K])
        s_keep = c.sem("e3_keep_staged")
        s_weight = c.sem("e3_weight_staged")
        s_tail = c.sem("e3_tail")
        s_zero = c.sem("e3_zeroed")

        @block.gpsimd
        def _(pool):
            e.gather(pool)

        @block.sync
        def _(sp):
            e.run(sp, lambda i, s, n: e.write_behind(sp, i, s, n, lambda *a: None))
            e.write_last(sp)

        @block.scalar
        def _(act):
            e.stage_first(act, g.pay[:, :, 0])

            def body(i, s, n):
                nc.scalar.copy(weight[:, s, 0:n], g.weight[:, bass.ds(2 * K * i + s * K, n)]).then_inc(s_weight, 1)
                e.wait_gathered(act, i, s, n)
                e.stage_next(act, g.pay[:, :, 0], i, s, n)
                e.wait_rows_out(act, i, s)
                if not isinstance(i, int) or i or s:
                    act.wait_ge(e.s_rows, 2 * K * i + (s - 1) * K + 1)
                act.wait_ge(s_weight, 2 * i + s + 1)
                for k in range(n):
                    ins = nc.scalar.activation(e.rows[:, s, k, :], e.gathered[:, s, k, :], ACT.Copy,
                                               scale=weight[:, s, k:k + 1])
                ins.then_inc(e.s_used, 1)
            act.wait_ge(s_zero, 1)
            e.run(act, body)

        @block.vector
        def _(dve):
            dve.memset(e.rows[:, 1, K - 1, :], 0.0).then_inc(s_zero, 1)
            dve.wait_ge(s_zero, 1)

            def body(i, s, n):
                dve.tensor_copy(keep[:, s, 0:n], g.keep[:, bass.ds(2 * K * i + s * K, n)]).then_inc(s_keep, 1)
                dve.wait_ge(s_keep, 2 * i + s + 1)
                dve.wait_ge(e.s_used, 2 * i + s + 1)
                e.sum_steps(dve, keep, i, s, n)
            e.run(dve, body)
            e.keep_ends(dve, g.tail[:, 0:D], s_tail)


def order_phase(nc, top, g):
    with top.phase() as c, nc.Block() as block:
        cum = c.ps("or_sums", [P, 4, 512])
        offset = c.sb("or_offset", [P, NT])
        end = c.sb("or_end", [P, NT])
        spare = c.sb("or_spare", [P, NT])
        trash = c.sb("or_trash", [P, NT])
        s_trash = c.sem("or_trash_ready")
        s_v = c.sem("or_vector_line")
        s_sum = c.sem("or_sums_ready")

        @block.gpsimd
        def _(pool):
            pool.iota(trash[:, :], [[P, NT]], base=E, channel_multiplier=1,
                      allow_small_or_imprecise_dtypes=True).then_inc(s_trash, 1)

        @block.tensor
        def _(pe):
            for n, hist in enumerate((g.src_hist, g.dst_hist)):
                pe.matmul(cum[:, 2 * n, 0:NT], g.upto[:, :], hist[:, :], start=True, stop=True)
                pe.matmul(cum[:, 2 * n + 1, 0:NT], g.ones[:, :], hist[:, :], start=True, stop=True).then_inc(s_sum, 1)

        @block.vector
        def _(dve):
            line = Line(dve, s_v)
            dve.wait_ge(s_trash, 1)
            for n, (hist, start, last, has) in enumerate(((g.src_hist, g.src_start, g.src_last, g.src_has),
                                                          (g.dst_hist, g.dst_start, g.dst_last, g.dst_has))):
                dve.wait_ge(s_sum, n + 1)
                line(dve.tensor_copy(end[:, :], cum[:, 2 * n + 1, 0:NT]))
                line(dve.tensor_tensor_scan(offset[:, :], g.ones[:, 0:NT], end[:, :], 0.0, ALU.mult, ALU.add))
                line(dve.tensor_tensor(offset[:, :], offset[:, :], end[:, :], ALU.subtract))
                line(dve.tensor_tensor(end[:, :], cum[:, 2 * n, 0:NT], offset[:, :], ALU.add))
                line(dve.tensor_tensor(start[:, :], end[:, :], hist[:, :], ALU.subtract))
                line(dve.memset(last[:, NT:NT + KN], 0))
                line(dve.tensor_scalar(last[:, 0:NT], end[:, :], -1.0, 0.0, ALU.add, ALU.max))
                line(dve.tensor_scalar(has[:, :], hist[:, :], 0.0, None, ALU.is_gt))
            line(dve.tensor_tensor(end[:, :], g.dst_start[:, :], trash[:, :], ALU.subtract))
            line(dve.tensor_tensor(end[:, :], end[:, :], g.dst_has[:, :], ALU.mult))
            line(dve.tensor_tensor(g.term_row[:, 0:NT], end[:, :], trash[:, :], ALU.add))


def sort_phase(nc, top, g, dram):
    with top.phase() as c, nc.Block() as block:
        row = c.sb("so_src_row", [P, 2, K, P], I32)
        pay = c.sb("so_payload", [P, 2, K, 2], I32)
        place = c.sb("so_place", [P, 2, K], I32)
        src = c.sb("so_src_stage", [P, 2, K])
        low = c.sb("so_low_hot", [P, 2, K, P], BF16)
        high = c.sb("so_high_hot", [P, 2, K, NT], BF16)
        low_t = c.sb("so_low_hot_transposed", [P, 2, K, P])
        count = c.sb("so_counts", [P, 2, NT])
        waste = c.sb("so_in_step_waste", [P, K, P])
        looked = c.sb("so_looked_waste", [P, K, NT])
        same = c.sb("so_in_step", [P, 2, K])
        before = c.sb("so_before", [P, K])
        flip = c.ps("so_low_flipped", [P, 2, 1024], BF16)
        table = c.ps("so_table", [P, 512])
        look = c.ps("so_looked_up", [P, 3, 512])
        look_at = lambda k: look[:, k // 4, (k % 4) * NT:(k % 4 + 1) * NT]
        s_row = [c.sem(f"so_row_loaded{s}") for s in range(2)]
        s_src = c.sem("so_src_staged")
        s_pay = c.sem("so_payload_staged")
        s_hot = c.sem("so_hot")
        s_same = c.sem("so_in_step_counted")
        s_flip = c.sem("so_flipped")
        s_low = c.sem("so_low_transposed")
        s_table = c.sem("so_table_counted")
        s_count = c.sem("so_table_copied")
        s_look = c.sem("so_lookups")
        s_before = c.sem("so_before_read")
        s_place = c.sem("so_places")
        s_sum = c.sem("so_places_summed")
        s_scat = [c.soft(f"so_scattered{s}") for s in range(2)]
        s_go = c.sem("so_scatter_go")

        later = lambda i: not isinstance(i, int) or i > 0

        def run(eng, prepare, place_all=None, behind=False):
            if place_all is None:
                batches(eng, NB, lambda i, s: prepare(i, s, K))
                prepare(NB // 2, 0, 1)
                return

            stages = [(prepare, 0), (place_all, 1)] if behind else [(place_all, 1), (prepare, 0)]

            def last():
                for stage, lag in stages:
                    stage(*((NB // 2 - 1, 1, K) if lag else (NB // 2, 0, 1)))
                place_all(NB // 2, 0, 1)
            lagged(eng, NB, [(lambda i, s, stage=stage: stage(i, s, K), lag) for stage, lag in stages], last)

        @block.gpsimd
        def _(pool):
            def scatter(i, s, n):
                pool.wait_ge(s_pay, 2 * i + s + 1)
                pool.wait_ge(s_place, 2 * i + s + 1)
                pool.sem_inc(s_go, 1)
                for k in range(n):
                    pool.indirect_dma_start(
                        out=dram.sorted[:, :], in_=pay[:, s, k, :], in_offset=None,
                        out_offset=bass.IndirectOffsetOnAxis(ap=place[:, s, k:k + 1], axis=0)).then_inc(s_scat[s], 16)
            run(pool, scatter)
            pool.wait_ge(s_scat[0], 16 * K * (NB // 2) + 16)
            pool.wait_ge(s_scat[1], 16 * K * (NB // 2))

        @block.sync
        def _(sp):
            def load(i, s, n):
                if later(i):
                    sp.wait_ge(s_same, K * (2 * i + s - 1))
                sp.dma_start(row[:, s, 0:n, :].rearrange("p k q -> p (k q)"),
                             dram.src_t[bass.ds(2 * K * i + s * K, n), :].rearrange("k q -> (k q)")
                             .partition_broadcast(P)).then_inc(s_row[s], 16)
            run(sp, load)

        @block.scalar
        def _(act):
            def prepare(i, s, n):
                act.wait_ge(s_flip, 2 * i + s + 1)
                if later(i):
                    act.wait_ge(s_look, 2 * K * i + (s - 1) * K)
                for a, e in ((0, min(n, 8)), (8, n)):
                    if a < e:
                        ins = nc.scalar.copy(low_t[:, s, a:e, :].rearrange("p k q -> p (k q)"),
                                             flip[:, a // 8, 0:(e - a) * P])
                ins.then_inc(s_low, 1)

            def place_all(i, s, n):
                b = 2 * K * i + s * K
                for k in range(n):
                    act.wait_ge(s_table, b + k + 1)
                    if later(i) or s or k >= 2:
                        act.wait_ge(s_look, b + k - 1)
                    nc.scalar.copy(count[:, (s * K + k) % 2, :], table[:, 0:NT]).then_inc(s_count, 1)
                if later(i):
                    act.wait_ge(s_scat[s], 16 * K * i)
                nc.scalar.copy(pay[:, s, 0:n, :], g.pay[:, bass.ds(2 * K * i + s * K, n), :]).then_inc(s_pay, 1)
            run(act, prepare, place_all)

        @block.vector
        def _(dve):
            def prepare(i, s, n):
                b = 2 * K * i + s * K
                dve.tensor_copy(src[:, s, 0:n], g.src[:, bass.ds(b, n)]).then_inc(s_src, 1)
                if later(i):
                    dve.wait_ge(s_table, b - K + 1)
                for digit, to, m in ((g.src_lo, low, P), (g.src_hi, high, NT)):
                    dve.tensor_tensor(to[:, s, 0:n, :], digit[:, bass.ds(b, n)].unsqueeze(2).to_broadcast([P, n, m]),
                                      g.rowb[:, 0:m].unsqueeze(1).to_broadcast([P, n, m]), ALU.is_equal).then_inc(s_hot, 1)
                dve.wait_ge(s_row[s], 16 * (i + 1))
                dve.wait_ge(s_src, 2 * i + s + 1)
                if later(i) or s:
                    dve.wait_ge(s_same, b)
                for k in range(n):
                    dve.scalar_tensor_tensor(out=waste[:, k, :], in0=row[:, s, k, :], scalar=src[:, s, k:k + 1],
                                             in1=g.after[:, :], op0=ALU.is_equal, op1=ALU.mult,
                                             accum_out=same[:, s, k:k + 1]).then_inc(s_same, 1)

            def place_all(i, s, n):
                b = 2 * K * i + s * K
                if later(i) or s:
                    dve.wait_ge(s_before, b)
                    dve.wait_ge(s_place, 2 * i + s)
                for k in range(n):
                    if k % 4 == 0:
                        dve.wait_ge(s_look, b + min(k + 4, n))
                    dve.scalar_tensor_tensor(out=looked[:, k, :], in0=look_at(k), scalar=1.0,
                                             in1=high[:, s, k, :], op0=ALU.mult, op1=ALU.mult,
                                             accum_out=before[:, k:k + 1]).then_inc(s_before, 1)
                if later(i):
                    dve.wait_ge(s_scat[s], 16 * K * i)
                dve.wait_ge(s_same, b + n)
                dve.wait_ge(s_before, b + n)
                ins = dve.tensor_tensor(place[:, s, 0:n], same[:, s, 0:n], before[:, 0:n], ALU.add)
                if n == K:
                    ins.then_inc(s_place, 1)
                else:
                    ins.then_inc(s_sum, 1)
                    dve.wait_ge(s_sum, 1)
                    dve.tensor_copy(place[LONG:P, s, 0:1], g.trash[LONG:P, :]).then_inc(s_place, 1)
            run(dve, prepare, place_all, behind=True)

        @block.tensor
        def _(pe):
            pe.matmul(table[:, 0:NT], g.ident[:, :], g.src_start[:, :], start=True, stop=False,
                      skip_group_check=True).then_inc(s_table, 1)

            def prepare(i, s, n):
                pe.wait_ge(s_hot, 4 * i + 2 * s + 2)
                if later(i) or s:
                    pe.wait_ge(s_low, 2 * i + s)
                for k in range(n):
                    ins = pe.transpose(flip[:, k // 8, (k % 8) * P:(k % 8 + 1) * P], low[:, s, k, :], g.identb[:, :])
                ins.then_inc(s_flip, 1)

            def place_all(i, s, n):
                b = 2 * K * i + s * K
                pe.wait_ge(s_low, 2 * i + s + 1)
                for k in range(n):
                    pe.wait_ge(s_count, b + k + 1)
                    pe.matmul(table[:, 0:NT], low[:, s, k, :], high[:, s, k, :], start=False, stop=False,
                              skip_group_check=True).then_inc(s_table, 1)
                    if k % 4 == 0 and (later(i) or s):
                        pe.wait_ge(s_before, b - K + min(k + 4, K))
                    pe.matmul(look_at(k), low_t[:, s, k, :], count[:, (s * K + k) % 2, :],
                              start=True, stop=True).then_inc(s_look, 1)
            run(pe, prepare, place_all)


def terms_phase(nc, top, g, dram):
    with top.phase() as c, nc.Block() as block:
        first = c.sb("te_first", [P, 1], I32)
        head = c.sb("te_head", [P, HEADS])
        s_first = c.sem("te_first_staged")
        s_clean = c.sem("te_last_step_zeroed")
        s_head = c.soft("te_head_gathered")
        s_load = c.sem("te_loaded")
        s_set = c.sem("te_heads_set")
        s_v = c.sem("te_vector_line")

        @block.sync
        def _(sp):
            sp.wait_ge(s_clean, 1)
            long, short = chunked(dram.dst_terms[0:E])
            sp.dma_start(g.sdst[0:LONG, 0:STEPS + 1, :], long).then_inc(s_load, 16)
            sp.dma_start(g.sdst[LONG:P, 0:STEPS, :], short).then_inc(s_load, 16)

        @block.gpsimd
        def _(pool):
            pool.wait_ge(s_first, 1)
            pool.indirect_dma_start(out=head[:, :], out_offset=None, in_=dram.node_terms[:, :],
                                    in_offset=bass.IndirectOffsetOnAxis(ap=first[:, :], axis=0)).then_inc(s_head, 16)

        @block.vector
        def _(dve):
            dve.tensor_copy(first[:, :], g.dst_seg.first[:, :]).then_inc(s_first, 1)
            dve.memset(g.sdst[:, STEPS, :], 0.0).then_inc(s_clean, 1)
            dve.wait_ge(s_head, 16)
            dve.wait_ge(s_load, 32)
            dve.tensor_copy(g.sdst[:, 0, :], head[:, :]).then_inc(s_set, 1)
            dve.wait_ge(s_set, 1)
            line = Line(dve, s_v)
            for h in range(HEADS):
                line(dve.tensor_tensor_scan(g.sdst[:, 0:STEPS + 1, h], g.keep[:, 0:STEPS + 1], g.sdst[:, 0:STEPS + 1, h],
                                            0.0, ALU.mult, ALU.add))


class SourceOrder:

    def __init__(self, c, g, dram):
        self.g, self.dram = g, dram
        T = STEPS + 1
        self.rel, self.up = c.sb("we_relation", [P, T]), c.sb("we_count_up", [P, T])
        self.in_first, self.in_last = g.spare[:, 0:T], g.spare[:, T:2 * T]
        self.heads = c.sb("we_first_counts", [P, REL])
        self.tails = c.sb("we_last_counts", [P, REL])
        self.others = c.sb("we_other_chunks", [P, 2, REL])
        self.ps = c.ps("we_carried", [P, 2, REL])
        self.bounds = Boundaries(c, g, "bs", g.src, g.src_seg, self.in_first)
        self.s_load = c.sem("we_edges_loaded")
        self.s_v = c.sem("we_vector_line")
        self.s_cnt = c.sem("we_counts_ready")
        self.s_ps = c.sem("we_carried_ready")

    def sync(self, sp):
        long, short = chunked(self.dram.sorted[0:E])
        sp.dma_start(self.g.pay[0:LONG, 0:STEPS + 1, :], long).then_inc(self.s_load, 16)
        sp.dma_start(self.g.pay[LONG:P, 0:STEPS, :], short).then_inc(self.s_load, 16)

    def vector(self, dve):
        g, T, seg = self.g, STEPS + 1, self.g.src_seg
        rel, up, heads, tails, others = self.rel, self.up, self.heads, self.tails, self.others
        line = Line(dve, self.s_v)
        dve.wait_ge(self.s_load, 32)
        line(dve.tensor_scalar(g.src[:, :], g.pay[:, :, 1], (1 << RSHIFT) - 1, None, ALU.bitwise_and))
        line(dve.tensor_tensor(g.keep[:, 1:W], g.src[:, 1:W], g.src[:, 0:W - 1], ALU.is_equal))
        self.bounds.vector(line)
        bits = up[:, :].bitcast(I32)
        line(dve.tensor_scalar(bits, g.pay[:, 0:T, 1], RSHIFT, None, ALU.logical_shift_right))
        line(dve.tensor_copy(rel[:, :], bits))
        line(dve.memset(rel[LONG:P, STEPS:T], -1.0))
        line(dve.tensor_scalar(self.in_last, g.src[:, 0:T], seg.last[:, 0:1], None, ALU.is_equal))
        for r in range(REL):
            for inside, counts in ((self.in_first, heads), (self.in_last, tails)):
                line(dve.scalar_tensor_tensor(out=up[:, :], in0=rel[:, :], scalar=float(r), in1=inside,
                                              op0=ALU.is_equal, op1=ALU.mult, accum_out=counts[:, r:r + 1]))
        dve.sem_inc(self.s_cnt, 1)
        dve.wait_ge(self.s_ps, 2)
        line(dve.tensor_copy(others[:, :, :], self.ps[:, :, :]))
        line(dve.memset(g.keep[:, 0:1], 1.0))
        line(dve.memset(g.keep[LONG:P, STEPS:STEPS + 1], 1.0))
        line(dve.memset(g.keep[:, STEPS + 1:STEPS + 2], 1.0))
        line(dve.memset(g.weight[:, :], 0.0))
        is_rel, down = self.in_first, self.in_last
        for r in range(REL):
            line(dve.tensor_scalar(is_rel, rel[:, :], float(r), None, ALU.is_equal))
            line(dve.tensor_tensor_scan(up[:, :], g.keep[:, 0:T], is_rel, others[:, 0, r:r + 1],
                                        ALU.mult, ALU.add))
            line(dve.tensor_tensor_scan(down[:, ::-1], g.keep[:, 1:T + 1][:, ::-1], is_rel[:, ::-1],
                                        others[:, 1, r:r + 1], ALU.mult, ALU.add))
            line(dve.scalar_tensor_tensor(out=up[:, :], in0=up[:, :], scalar=-1.0, in1=down,
                                          op0=ALU.add, op1=ALU.add))
            line(dve.tensor_tensor(up[:, :], up[:, :], is_rel, ALU.mult))
            line(dve.tensor_tensor(g.weight[:, 0:T], g.weight[:, 0:T], up[:, :], ALU.add))
        line(dve.tensor_scalar(g.weight[:, :], g.weight[:, :], 1.0, None, ALU.max))
        line(dve.reciprocal(g.weight[:, :], g.weight[:, :]))
        line(dve.memset(g.keep[:, 0:1], 0.0))

    def tensor(self, pe, batch):
        if batch == 0:
            self.bounds.tensor(pe)
        elif batch == 2:
            seg = self.g.src_seg
            pe.wait_ge(self.s_cnt, 1)
            pe.matmul(self.ps[:, 0, :], seg.carry_mask[:, :], self.tails[:, :], start=True, stop=True).then_inc(self.s_ps, 1)
            pe.matmul(self.ps[:, 1, :], seg.carry_mask_t[:, :], self.heads[:, :], start=True, stop=True).then_inc(self.s_ps, 1)


def carry_phase(nc, top, g, tag, rows, seg, attention=False):
    width = AW if attention else D
    with top.phase() as c, nc.Block() as block:
        index = c.sb(f"{tag}_index", [P, 1], I32)
        row = c.sb(f"{tag}_row", [P, width])
        new = c.sb(f"{tag}_new_row", [P, width])
        carried = c.ps(f"{tag}_carried", [P, 512])
        s_index = c.sem(f"{tag}_index_ready")
        s_row = c.soft(f"{tag}_row_gathered")
        s_sum = c.sem(f"{tag}_carried_summed")
        s_new = c.sem(f"{tag}_new_row_ready")
        s_out = c.soft(f"{tag}_row_written")
        if attention:
            diag = c.sb(f"{tag}_diag", [P, HEADS, P])
            open_t = c.sb(f"{tag}_open", [P, P])
            score = c.sb(f"{tag}_scores", [P, HEADS, P])
            share = c.sb(f"{tag}_shares", [P, HEADS, P])
            share_t = c.sb(f"{tag}_shares_transposed", [P, HEADS, P])
            m = c.sb(f"{tag}_max", [P, HEADS])
            own = c.sb(f"{tag}_own", [P, HEADS])
            spread = c.ps(f"{tag}_spread", [P, HEADS, P])
            flipped = c.ps(f"{tag}_flipped", [P, HEADS, P])
            s_v = c.sem(f"{tag}_vector_line")
            s_diag = c.sem(f"{tag}_diagonals")
            s_spread = c.sem(f"{tag}_max_spread")
            s_score = c.sem(f"{tag}_exponents_ready")
            s_share = c.sem(f"{tag}_shares_ready")
            s_flip = c.sem(f"{tag}_shares_flipped")
            s_st = c.sem(f"{tag}_shares_copied")
            tail = g.tail[:, :].rearrange("p (h w) -> p h w", h=HEADS)
            row_h = row[:, :].rearrange("p (h w) -> p h w", h=HEADS)
            new_h = new[:, :].rearrange("p (h w) -> p h w", h=HEADS)

        @block.gpsimd
        def _(pool):
            pool.wait_ge(s_index, 1)
            pool.indirect_dma_start(out=row[:, :], out_offset=None, in_=rows,
                                    in_offset=bass.IndirectOffsetOnAxis(ap=index[:, :], axis=0)).then_inc(s_row, 16)
            pool.wait_ge(s_new, 1)
            pool.indirect_dma_start(out=rows, in_=new[:, :], in_offset=None,
                                    out_offset=bass.IndirectOffsetOnAxis(ap=index[:, :], axis=0)).then_inc(s_out, 16)
            pool.wait_ge(s_out, 16)

        @block.vector
        def _(dve):
            dve.tensor_copy(index[:, :], seg.first_end[:, :]).then_inc(s_index, 1)
            if not attention:
                dve.wait_ge(s_row, 16)
                dve.wait_ge(s_sum, 1)
                dve.tensor_tensor(new[:, :], row[:, :], carried[:, 0:D], ALU.add).then_inc(s_new, 1)
                return
            line = Line(dve, s_v)
            for h in range(HEADS):
                ins = dve.tensor_scalar(diag[:, h, :], g.ident[:, :], tail[:, h, HD + 1:HD + 2], None, ALU.mult)
            ins.then_inc(s_diag, 1)
            line(dve.tensor_scalar(open_t[:, :], seg.carry_mask_t[:, :], -1.0, FAR, ALU.add, ALU.mult))
            dve.wait_ge(s_spread, 1)
            line(dve.tensor_tensor(score[:, :, :], spread[:, :, :],
                                   open_t[:, :].unsqueeze(1).to_broadcast([P, HEADS, P]), ALU.add))
            line(dve.tensor_reduce(m[:, :], score[:, :, :], AX.X, ALU.max))
            dve.wait_ge(s_row, 16)
            line(dve.tensor_tensor(m[:, :], m[:, :], row_h[:, :, HD + 1], ALU.max))
            line(dve.tensor_tensor(own[:, :], row_h[:, :, HD + 1], m[:, :], ALU.subtract))
            dve.tensor_tensor(score[:, :, :], score[:, :, :], m[:, :].unsqueeze(2).to_broadcast([P, HEADS, P]),
                              ALU.subtract).then_inc(s_score, 1)
            dve.wait_ge(s_flip, 1)
            dve.tensor_copy(share_t[:, :, :], flipped[:, :, :]).then_inc(s_st, 1)
            dve.wait_ge(s_sum, 1)
            dve.wait_ge(s_share, 2)
            line(dve.tensor_copy(new[:, :], row[:, :]))
            line(dve.tensor_tensor(new_h[:, :, 0:HD + 1], row_h[:, :, 0:HD + 1],
                                   own[:, :].unsqueeze(2).to_broadcast([P, HEADS, HD + 1]), ALU.mult))
            dve.tensor_tensor(new_h[:, :, 0:HD + 1], new_h[:, :, 0:HD + 1],
                              carried[:, 0:HEADS * (HD + 1)].rearrange("p (h w) -> p h w", h=HEADS),
                              ALU.add).then_inc(s_new, 1)

        @block.scalar
        def _(act):
            if attention:
                act.wait_ge(s_score, 1)
                nc.scalar.activation(share[:, :, :], score[:, :, :], ACT.Exp).then_inc(s_share, 1)
                nc.scalar.activation(own[:, :], own[:, :], ACT.Exp).then_inc(s_share, 1)

        @block.tensor
        def _(pe):
            if not attention:
                pe.matmul(carried[:, 0:D], seg.carry_mask[:, :], g.tail[:, 0:D], start=True, stop=True).then_inc(s_sum, 1)
                return
            pe.wait_ge(s_diag, 1)
            pe.matmul(spread[:, :, :].rearrange("p h q -> p (h q)"), g.ones[:, :],
                      diag[:, :, :].rearrange("p h q -> p (h q)"), start=True, stop=True).then_inc(s_spread, 1)
            pe.wait_ge(s_share, 1)
            for h in range(HEADS):
                ins = pe.transpose(flipped[:, h, :], share[:, h, :], g.ident[:, :])
            ins.then_inc(s_flip, 1)
            pe.wait_ge(s_st, 1)
            for h in range(HEADS):
                ins = pe.matmul(carried[:, h * (HD + 1):(h + 1) * (HD + 1)], share_t[:, h, :], tail[:, h, 0:HD + 1],
                                start=True, stop=True)
            ins.then_inc(s_sum, 1)


def update_phase(nc, top, g, layer, rows, last, has, dram):
    tag = f"u{layer}"
    width = AW if layer == 2 else D
    with top.phase() as c, nc.Block() as block:
        index = c.sb(f"{tag}_index", [P, 2, KN], I32)
        got = c.sb(f"{tag}_gathered", [P, 2, KN, width])
        near = c.sb(f"{tag}_neighbours", [P, 2, KN, D])
        s_index = c.sem(f"{tag}_index_staged")
        s_got = [c.soft(f"{tag}_gathered{s}") for s in range(2)]
        s_go = c.sem(f"{tag}_gather_go")
        s_used = c.sem(f"{tag}_gathered_used")
        s_add = c.sem(f"{tag}_added")
        s_st = c.sem(f"{tag}_stats")
        s_root = c.sem(f"{tag}_root")
        s_n = c.sem(f"{tag}_norm_line")
        s_h = c.sem(f"{tag}_h_ready")
        s_in = c.sem(f"{tag}_inputs_ready")
        s_t = c.sem(f"{tag}_transposed")
        s_tc = c.sem(f"{tag}_transposes_copied")
        s_m = c.sem(f"{tag}_products_ready")
        s_v = c.sem(f"{tag}_vector_line")
        s_z = c.sem(f"{tag}_hidden_ready")
        s_zb = c.sem(f"{tag}_hidden_biased")
        s_zl = c.sem(f"{tag}_hidden_activated")
        s_out = c.sem(f"{tag}_x_out")
        flat = lambda ap: ap.rearrange("p k d -> p (k d)")
        if layer < 2:
            h = c.sb(f"{tag}_h", [P, 2, KN, D])
            ins_t = c.sb(f"{tag}_inputs_transposed", [P, 2, 2, KN * D])
            hid = c.sb(f"{tag}_hidden", [P, 2, KN * D])
            hid_a = c.sb(f"{tag}_hidden_act", [P, 2, KN * D])
            tp = c.ps(f"{tag}_transposes", [P, 2 - layer, 1024])
            mm = c.ps(f"{tag}_products", [P, 2, 1024])
            s_b = c.sem(f"{tag}_biased")
            if layer == 0:
                biased = c.sb(f"{tag}_biased_products", [P, KN, D])
            if layer == 1:
                zz = c.ps(f"{tag}_hidden_products", [P, 1024])
        if layer == 2:
            den = c.sb(f"{tag}_denominator", [P, KN, HEADS])
            neg = c.sb(f"{tag}_negative_part", [P, 2, KN * D])
            s_v2 = c.sem(f"{tag}_sum_line")
        later = lambda i: not isinstance(i, int) or i > 0
        at = lambda i, s: 2 * i + s

        @block.gpsimd
        def _(pool):
            def body(i, s):
                pool.wait_ge(s_index, at(i, s) + 1)
                if later(i):
                    pool.wait_ge(s_used, at(i, s) - 1)
                pool.sem_inc(s_go, 1)
                for k in range(KN):
                    pool.indirect_dma_start(
                        out=got[:, s, k, :], out_offset=None, in_=rows,
                        in_offset=bass.IndirectOffsetOnAxis(ap=index[:, s, k:k + 1], axis=0)).then_inc(s_got[s], 16)
            batches(pool, NNB, body)

        @block.scalar
        def _(act):
            def fetch(i, s):
                if not later(i) and not s:
                    nc.scalar.copy(index[:, 0, :], last[:, 0:KN]).then_inc(s_index, 1)
                else:
                    act.wait_ge(s_got[1 - s], 16 * KN * (i + s))
                nc.scalar.copy(index[:, 1 - s, :], last[:, bass.ds(KN * (2 * i + s + 1), KN)]).then_inc(s_index, 1)

            def norm(i, s):
                if layer < 2:
                    if later(i):
                        act.wait_ge(s_in if layer else s_t, at(i, s) - 1)
                    for k in range(KN):
                        normalise(nc, g, h[:, s], KN * at(i, s), k, s_h)

            def bias_hidden(i, s):
                act.wait_ge(s_z, at(i, s) + 1)
                if later(i):
                    act.wait_ge(s_zl, at(i, s) - 1)
                for a, b in GN:
                    ins = nc.scalar.activation(hid[:, s, a * D:b * D], zz[:, a * D:b * D], ACT.Identity, bias=g.b1[:, 0:1])
                ins.then_inc(s_zb, 1)

            def exponents(i, s):
                act.wait_ge(s_in, at(i, s) + 1)
                nc.scalar.activation(neg[:, s, :], neg[:, s, :], ACT.Exp).then_inc(s_zb, 1)
            lagged(act, NNB, [(norm, 0), (fetch, 0)] + {1: [(bias_hidden, 1)], 2: [(exponents, 1)]}.get(layer, []))
            if layer < 3:
                act.wait_ge(s_n, 6)
                nc.scalar.activation(g.shift[:, :], g.scale[:, :], ACT.Sqrt).then_inc(s_root, 1)

        @block.vector
        def _(dve):
            line, line2 = Line(dve, s_v), Line(dve, s_v2) if layer == 2 else None
            columns = lambda i, s: bass.ds(2 * KN * i + s * KN, KN)

            def take(i, s):
                dve.wait_ge(s_got[s], 16 * KN * (i + 1))
                if later(i):
                    dve.wait_ge(s_t if layer < 2 else s_add, at(i, s) - 1)
                has_b = has[:, columns(i, s)].unsqueeze(2)
                if layer != 2:
                    dve.tensor_tensor(near[:, s, :, :], got[:, s, :, :], has_b.to_broadcast([P, KN, D]),
                                      ALU.mult).then_inc(s_used, 1)
                if layer == 1:
                    dve.wait_ge(s_used, at(i, s) + 1)
                    dve.wait_ge(s_h, KN * (at(i, s) + 1))
                    dve.scalar_tensor_tensor(out=near[:, s, :, :], in0=h[:, s, :, :], scalar=2.0, in1=near[:, s, :, :],
                                             op0=ALU.mult, op1=ALU.add).then_inc(s_in, 1)
                    x = g.x[:, columns(i, s), :]
                    dve.tensor_tensor(x, x, g.bias_rows[:, 2, :].unsqueeze(1).to_broadcast([P, KN, D]),
                                      ALU.add).then_inc(s_b, 1)
                if layer == 2:
                    line.at(3 * at(i, s))
                    r = got[:, s, :, :].rearrange("p k (h w) -> p k h w", h=HEADS)
                    line(dve.tensor_scalar(den[:, :, :], r[:, :, :, HD], 1e-8, None, ALU.add))
                    line(dve.reciprocal(den[:, :, :], den[:, :, :]))
                    line(dve.tensor_tensor(den[:, :, :], den[:, :, :], has_b.to_broadcast([P, KN, HEADS]), ALU.mult))
                    dve.tensor_tensor(near[:, s, :, :].rearrange("p k (h w) -> p (k h) w", h=HEADS),
                                      r[:, :, :, 0:HD].rearrange("p k h w -> p (k h) w"),
                                      den[:, :, :].rearrange("p k h -> p (k h)").unsqueeze(2)
                                      .to_broadcast([P, KN * HEADS, HD]), ALU.mult).then_inc(s_used, 1)
                    dve.wait_ge(s_used, at(i, s) + 1)
                    dve.tensor_scalar(neg[:, s, :], flat(near[:, s, :, :]), 0.0, None, ALU.min).then_inc(s_in, 1)

            def copy_transposes(i, s):
                dve.wait_ge(s_t, at(i, s) + 1)
                if later(i):
                    dve.wait_ge(s_z if layer else s_m, at(i, s) - 1)
                ins = dve.tensor_copy(ins_t[:, s, 0, :], tp[:, 0, 0:KN * D])
                if layer == 0:
                    ins = dve.tensor_copy(ins_t[:, s, 1, :], tp[:, 1, 0:KN * D])
                ins.then_inc(s_tc, 1)

            def activate_hidden(i, s):
                dve.wait_ge(s_zb, at(i, s) + 1)
                if later(i):
                    dve.wait_ge(s_m, at(i, s) - 1)
                dve.scalar_tensor_tensor(out=hid_a[:, s, :], in0=hid[:, s, :], scalar=0.01, in1=hid[:, s, :],
                                         op0=ALU.mult, op1=ALU.max).then_inc(s_zl, 1)

            def add(i, s):
                x = flat(g.x[:, columns(i, s), :])
                if layer == 0:
                    dve.wait_ge(s_m, at(i, s) + 1)
                    dve.tensor_tensor(biased[:, :, :], mm[:, s, 0:KN * D].rearrange("p (k d) -> p k d", k=KN),
                                      g.bias_rows[:, 1, :].unsqueeze(1).to_broadcast([P, KN, D]), ALU.add).then_inc(s_b, 1)
                    dve.wait_ge(s_b, at(i, s) + 1)
                    dve.scalar_tensor_tensor(out=x, in0=flat(biased[:, :, :]), scalar=0.0, in1=x,
                                             op0=ALU.max, op1=ALU.add).then_inc(s_add, 1)
                elif layer == 1:
                    dve.wait_ge(s_m, at(i, s) + 1)
                    dve.wait_ge(s_b, at(i, s) + 1)
                    dve.tensor_tensor(x, mm[:, s, 0:KN * D], x, ALU.add).then_inc(s_add, 1)
                elif layer == 2:
                    line2.at(2 * at(i, s))
                    v = flat(near[:, s, :, :])
                    dve.wait_ge(s_zb, at(i, s) + 1)
                    line2(dve.scalar_tensor_tensor(out=v, in0=v, scalar=0.0, in1=neg[:, s, :], op0=ALU.max, op1=ALU.add))
                    line2(dve.tensor_scalar(v, v, -1.0, None, ALU.add))
                    dve.tensor_tensor(x, x, v, ALU.add).then_inc(s_add, 1)
                else:
                    dve.wait_ge(s_used, at(i, s) + 1)
                    dve.scalar_tensor_tensor(out=x, in0=flat(near[:, s, :, :]), scalar=0.0, in1=x,
                                             op0=ALU.max, op1=ALU.add).then_inc(s_add, 1)
                if layer < 3:
                    dve.wait_ge(s_add, at(i, s) + 1)
                    for k in range(KN):
                        one = bass.ds(2 * KN * i + s * KN + k, 1)
                        ins = dve.bn_stats(g.stats[:, one, :], g.x[:, one, :])
                    ins.then_inc(s_st, 1)
            lagged(dve, NNB, [(take, 0)] + {0: [(add, 2), (copy_transposes, 0)],
                                            1: [(activate_hidden, 1), (copy_transposes, 0), (add, 2)],
                                            2: [(add, 1)], 3: [(add, 0)]}[layer])
            if layer < 3:
                dve.wait_ge(s_st, NNB)
                norm_stats(Line(dve, s_n), lambda: dve.wait_ge(s_root, 1), g)

        @block.tensor
        def _(pe):
            if layer >= 2:
                return

            def transposes(i, s):
                if later(i) or s:
                    pe.wait_ge(s_tc, at(i, s))
                if layer == 0:
                    pe.wait_ge(s_h, KN * (at(i, s) + 1))
                    pe.wait_ge(s_used, at(i, s) + 1)
                else:
                    pe.wait_ge(s_in, at(i, s) + 1)
                for k in range(KN):
                    if layer == 0:
                        pe.transpose(tp[:, 1, k * D:(k + 1) * D], h[:, s, k, :], g.ident[:, :])
                    ins = pe.transpose(tp[:, 0, k * D:(k + 1) * D], near[:, s, k, :], g.ident[:, :])
                ins.then_inc(s_t, 1)

            def hidden(i, s):
                pe.wait_ge(s_tc, at(i, s) + 1)
                if later(i) or s:
                    pe.wait_ge(s_zb, at(i, s))
                for a, b in GN:
                    ins = pe.matmul(zz[:, a * D:b * D], g.w1[:, :], ins_t[:, s, 0, a * D:b * D], start=True, stop=True)
                ins.then_inc(s_z, 1)

            def products(i, s):
                pe.wait_ge(s_zl if layer else s_tc, at(i, s) + 1)
                if later(i):
                    pe.wait_ge(s_add, at(i, s) - 1)
                for k in range(KN):
                    to = mm[:, s, k * D:(k + 1) * D]
                    part = slice(k * D, (k + 1) * D)
                    if layer == 0:
                        pe.matmul(to, ins_t[:, s, 1, part], g.w0_h[:, :], start=True, stop=False)
                        ins = pe.matmul(to, ins_t[:, s, 0, part], g.w0_near[:, :], start=False, stop=True)
                    else:
                        ins = pe.matmul(to, hid_a[:, s, part], g.w2[:, :], start=True, stop=True)
                ins.then_inc(s_m, 1)
            lagged(pe, NNB, [(transposes, 0)] + ([(hidden, 0)] if layer else []) + [(products, 1)])

        @block.sync
        def _(sp):
            if layer != 3:
                return

            def write(i, s):
                sp.wait_ge(s_add, at(i, s) + 1)
                sp.dma_start(nodes(dram.out[0:(NT - 1) * P, :])[:, bass.ds(KN * at(i, s), KN), :],
                             g.x[:, bass.ds(KN * at(i, s), KN), :]).then_inc(s_out, 16)
            batches(sp, NNB - 2, write)
            write(NNB // 2 - 1, 0)
            sp.wait_ge(s_add, NNB)
            sp.dma_start(nodes(dram.out[0:(NT - 1) * P, :])[:, NT - KN:NT - 1, :], g.x[:, NT - KN:NT - 1, :]).then_inc(s_out, 16)
            sp.dma_start(dram.out[(NT - 1) * P:N, :], g.x[0:TAIL, NT - 1, :]).then_inc(s_out, 16)
            sp.wait_ge(s_out, 16 * (NNB + 1))


class Names:
    pass


def segments(top, tag):
    seg = Names()
    seg.first, seg.last, seg.first_end = (top.sb(f"{tag}_{n}", [P, 1]) for n in ("first", "last", "first_end"))
    seg.carry_mask, seg.carry_mask_t = (top.sb(f"{tag}_{n}", [P, P]) for n in ("carry_mask", "carry_mask_t"))
    return seg


def build(nc, dram):
    with ExitStack() as ctx:
        top = Core(nc, ctx)
        top.shared = ctx
        g = Names()
        g.x = top.sb("x", [P, NT, D])
        g.src, g.dst = top.sb("src", [P, W], I32), top.sb("dst", [P, W], I32)
        g.pay = top.sb("payload", [P, W, 2], I32)
        g.keep = top.sb("keep", [P, W])
        turns = top.sb("edge_turns", [P, (STEPS + 1) * HEADS])
        g.src_lo, g.src_hi, g.dst_lo, g.dst_hi = (turns[:, n * W // 2:(n + 1) * W // 2].bitcast(BF16) for n in range(4))
        g.sdst = turns[:, :].rearrange("p (t h) -> p t h", h=HEADS)
        g.weight = turns[:, 0:W]
        g.spare = turns[:, W:]
        g.stats = top.sb("stats", [P, NT, 6])
        g.mean, g.scale, g.shift = (top.sb(n, [P, NT]) for n in ("mean_sum", "norm_scale", "norm_shift"))
        g.ident, g.ones, g.before, g.upto, g.after, g.row = (
            top.sb(n, [P, P]) for n in ("ident", "ones", "before", "upto", "after", "row_numbers"))
        g.identb, g.rowb = top.sb("ident_bf16", [P, P], BF16), top.sb("row_numbers_bf16", [P, P], BF16)
        g.part, g.chunk_start = top.sb("partition_number", [P, 1]), top.sb("chunk_start", [P, 1])
        g.trash = top.sb("trash_row", [P, 1], I32)
        g.tail = top.sb("chunk_ends", [P, AW])
        g.src_hist, g.dst_hist, g.src_start, g.dst_start, g.src_has, g.dst_has = (
            top.sb(n, [P, NT]) for n in ("src_hist", "dst_hist", "src_start", "dst_start", "src_has", "dst_has"))
        g.src_last, g.dst_last, g.term_row = (top.sb(n, [P, NT + KN], I32) for n in ("src_last", "dst_last", "term_row"))
        g.w0_edge = top.sb("w0_edge", [DE, D])
        g.w0_node, g.w0_h, g.w0_near, g.w1, g.w2 = (top.sb(n, [P, D]) for n in ("w0_node", "w0_h", "w0_near", "w1", "w2"))
        g.b0_msg, g.b0_apply, g.b2 = (top.sb(n, [1, D]) for n in ("b0_msg", "b0_apply", "b2"))
        g.b1 = top.sb("b1", [P, 1])
        g.wx = top.sb("wx", [P, D + 2 * HEADS])
        g.w_att, g.a_cols = top.sb("w_att", [P, D]), top.sb("a_columns", [P, 2 * HEADS])
        g.w3 = top.sb("w3", [P, REL * D])
        g.bias_rows = top.sb("bias_rows", [P, 3, D])
        g.dst_seg, g.src_seg = segments(top, "dst_segments"), segments(top, "src_segments")

        scratch = lambda n, shape, dt=F32: nc.dram_tensor(n, shape, dt).ap()
        dram.table0 = scratch("node_table", [NPAD, D])
        dram.table2 = scratch("attention_table", [NPAD, AW])
        dram.table3 = scratch("relation_table", [REL * NPAD, D])
        dram.rows = scratch("segment_rows", [E, D])
        dram.rows2 = scratch("attention_rows", [E, AW])
        dram.sorted = scratch("sorted_edges", [E + P, 2], I32)
        dram.dst_terms = scratch("dst_terms", [E + NPAD, HEADS])
        dram.node_terms = scratch("node_terms_rows", [NPAD, HEADS])

        setup_phase(nc, top, g, dram)
        boundary_phase(nc, top, g, dram)
        by_column = lambda table: lambda j, k: nodes(table)[:, bass.ds(j, k), :]
        project_phase_0(nc, top, g, dram)
        edge_phase_0(nc, top, g, dram)
        order_phase(nc, top, g)
        sort_phase(nc, top, g, dram)
        carry_phase(nc, top, g, "c0", dram.rows[:, :], g.dst_seg)
        update_phase(nc, top, g, 0, dram.rows[:, :], g.dst_last, g.dst_has, dram)
        norm_phase_1(nc, top, g, dram)
        edge_phase_1(nc, top, g, dram)
        carry_phase(nc, top, g, "c1", dram.rows[:, :], g.dst_seg)
        update_phase(nc, top, g, 1, dram.rows[:, :], g.dst_last, g.dst_has, dram)

        heads = lambda ap: ap.rearrange("p (h w) -> p h w", h=HEADS)

        def ones_column(dve, out, ready):
            dve.memset(out[:, :, :, :].rearrange("p s k (h w) -> p (s k h) w", h=HEADS)[:, :, HD], 1.0).then_inc(ready, 1)

        def scores(to, ps):
            return nc.vector.tensor_copy(heads(to)[:, :, HD + 1], ps[:, 512:512 + HEADS])
        project_phase(nc, top, g, "p2", by_column(dram.table2), g.wx, D + 2 * HEADS, AW,
                      copy_act=lambda to, ps: nc.scalar.copy(heads(to)[:, :, 0:HD], heads(ps[:, 0:D])),
                      copy_dve=scores, prepare=ones_column, terms=dram)
        terms_phase(nc, top, g, dram)
        edge_phase_2(nc, top, g, dram)
        carry_phase(nc, top, g, "c2", dram.rows2[:, :], g.dst_seg, attention=True)
        update_phase(nc, top, g, 2, dram.rows2[:, :], g.dst_last, g.dst_has, dram)

        by_relation = lambda j, k: dram.table3.rearrange("(r j p) d -> p r j d", r=REL, p=P)[:, :, bass.ds(j, 1), :].rearrange(
            "p r j d -> p r (j d)")
        project_phase(nc, top, g, "p3", by_relation, g.w3, REL * D, REL * D,
                      copy_act=lambda to, ps: nc.scalar.copy(to, ps[:, 0:REL * D]),
                      beside=lambda c: SourceOrder(c, g, dram))
        edge_phase_3(nc, top, g, dram)
        carry_phase(nc, top, g, "c3", dram.rows[:, :], g.src_seg)
        update_phase(nc, top, g, 3, dram.rows[:, :], g.src_last, g.src_has, dram)


def kernel(x, src, dst, edge_attr_128, edge_attr_64, edge_type_8, L0_gnn_W_msg_w, L0_gnn_W_msg_b, L0_gnn_W_apply_w,
           L0_gnn_W_apply_b, L1_gnn_W1, L1_gnn_b1, L1_gnn_W2, L1_gnn_b2, L2_gnn_W, L2_gnn_a_w, L3_gnn_weights):
    import numpy as np
    import concourse.bacc as bacc
    from concourse.bass_utils import run_bass_kernel_spmd

    cut = LONG * (STEPS + 1)

    def by_step(a):
        out = np.zeros((P, STEPS + 1) + a.shape[1:], a.dtype)
        out[:LONG] = a[:cut].reshape((LONG, STEPS + 1) + a.shape[1:])
        out[LONG:, :STEPS] = a[cut:].reshape((P - LONG, STEPS) + a.shape[1:])
        return out.transpose(2, 1, 0)

    arr = lambda a: np.asarray(a)
    src_a = arr(src)
    w_msg, w_app, w_rel = arr(L0_gnn_W_msg_w), arr(L0_gnn_W_apply_w), arr(L3_gnn_weights)
    given = {
        "x": arr(x), "src": src_a, "dst": arr(dst), "edge_type_8": arr(edge_type_8),
        "edge_attr_128": arr(edge_attr_128), "edge64_t": by_step(arr(edge_attr_64)),
        "src_t": by_step(src_a[:, None])[0],
        "w0_node": w_msg[:, :D].T, "w0_edge": w_msg[:, D:].T, "b0_msg": arr(L0_gnn_W_msg_b)[None, :],
        "w0_h": w_app[:, :D].T, "w0_near": w_app[:, D:].T, "b0_apply": arr(L0_gnn_W_apply_b)[None, :],
        "w1": arr(L1_gnn_W1), "b1": arr(L1_gnn_b1)[:, None], "w2": arr(L1_gnn_W2), "b2": arr(L1_gnn_b2)[None, :],
        "w_att": arr(L2_gnn_W), "w_att_t": arr(L2_gnn_W).T, "a_w": arr(L2_gnn_a_w)[:, None],
        "w3": w_rel.transpose(2, 0, 1).reshape(D, REL * D),
    }
    nc = bacc.Bacc("TRN2", target_bir_lowering=False, num_devices=1)
    dram, arrays = Names(), {}
    for name, a in given.items():
        a = np.ascontiguousarray(a)
        arrays[f"in_{name}"] = a
        ap = nc.dram_tensor(f"in_{name}", a.shape, mybir.dt.from_np(a.dtype), kind="ExternalInput").ap()
        dram.__dict__[name] = ap
    dram.out = nc.dram_tensor("out_x", (N, D), F32, kind="ExternalOutput").ap()
    build(nc, dram)
    r = run_bass_kernel_spmd(nc, [arrays], core_ids=[0])
    return r.results[0]["out_x"]
```
